# Optimizing a Trainium2 kernel written in Bass

```python
import numpy as np
import jax
import jax.numpy as jnp

def _softmax(x, axis=-1):
    return jax.nn.softmax(x, axis=axis)

def _gelu(x):
    return jax.nn.gelu(x, approximate=True)

def _silu(x):
    return jax.nn.silu(x)

def _sigmoid(x):
    return jax.nn.sigmoid(x)

def _layernorm(x, axis=-1, eps=1e-05):
    m = jnp.mean(x, axis=axis, keepdims=True)
    v = jnp.var(x, axis=axis, keepdims=True)
    return (x - m) / jnp.sqrt(v + eps)

def _scatter_add(tgt, idx, src, axis=0):
    return tgt.at[idx].add(src)

def _segment_sum(src, seg, n):
    return jax.ops.segment_sum(src, seg, n)
kernel_name = 'mk_gnn_preln_d4_gnn_r8_590751'

def setup_inputs(seed: int=0):
    np.random.seed(seed)
    _w = jnp.asarray

    def _rec_inputs():
        import jax
        import jax.numpy as jnp
        _gk = jax.random.key(seed)
        x = -0.0001006 + 1 * jax.random.normal(jax.random.fold_in(_gk, 1), (6250, 96), jnp.float32)
        src = jax.random.randint(jax.random.fold_in(_gk, 2), (200000,), 0, 6250, jnp.int32)
        dst = jax.random.randint(jax.random.fold_in(_gk, 3), (200000,), 0, 6250, jnp.int32)
        _o = jnp.argsort(dst, stable=True)
        src = src[_o]
        dst = dst[_o]
        edge_attr_32 = 0.000196303 + 1.00016 * jax.random.normal(jax.random.fold_in(_gk, 12), (200000, 32), jnp.float32)
        return (x, src, dst, edge_attr_32)
    x, src, dst, edge_attr_32 = _rec_inputs()

    def _L0_gnn_setup():
        import jax, jax.numpy as jnp
        import numpy as np
        N = 6250
        E = 100000
        D = 96
        EPS = 1e-05

        def layer_norm(x, w, b):
            mu = jnp.mean(x, axis=-1, keepdims=True)
            var = jnp.var(x, axis=-1, keepdims=True)
            return (x - mu) / jnp.sqrt(var + EPS) * w + b

        def gcn_conv(x, W, b, row, col, n):
            h = x @ W
            loops = jnp.arange(n, dtype=row.dtype)
            row2 = jnp.concatenate([row, loops])
            col2 = jnp.concatenate([col, loops])
            deg = jax.ops.segment_sum(jnp.ones(row2.shape[0], dtype=h.dtype), col2, num_segments=n)
            dinv = jnp.where(deg > 0, deg ** (-0.5), 0.0)
            norm = dinv[row2] * dinv[col2]
            out = jax.ops.segment_sum(h[row2] * norm[:, None], col2, num_segments=n)
            return out + b
        key = jax.random.key(seed)
        ks = jax.random.split(key, 8)
        x = jax.random.normal(ks[0], (N, D), dtype=jnp.float32)
        edge_index = jax.random.randint(ks[1], (2, E), 0, N, dtype=jnp.int64)
        s = 1.0 / np.sqrt(D)
        W1 = jax.random.uniform(ks[2], (D, D), minval=-s, maxval=s, dtype=jnp.float32)
        W2 = jax.random.uniform(ks[3], (D, D), minval=-s, maxval=s, dtype=jnp.float32)
        b1 = jnp.zeros((D,), dtype=jnp.float32)
        b2 = jnp.zeros((D,), dtype=jnp.float32)
        ln_in_w = jnp.ones((D,), dtype=jnp.float32)
        ln_in_b = jnp.zeros((D,), dtype=jnp.float32)
        ln_out_w = jnp.ones((D,), dtype=jnp.float32)
        ln_out_b = jnp.zeros((D,), dtype=jnp.float32)
        return {'x': x, 'edge_index': edge_index, 'W1': W1, 'b1': b1, 'W2': W2, 'b2': b2, 'ln_in_w': ln_in_w, 'ln_in_b': ln_in_b, 'ln_out_w': ln_out_w, 'ln_out_b': ln_out_b}
    _L0_gnn_all = _L0_gnn_setup()
    _L0_gnn_in = {k: v for k, v in _L0_gnn_all.items() if k in ('W1', 'b1', 'W2', 'b2', 'ln_in_w', 'ln_in_b', 'ln_out_w', 'ln_out_b')}
    del _L0_gnn_all

    def _L1_gnn_setup():
        import jax, jax.numpy as jnp
        import numpy as np
        N, E, D = (6250, 100000, 96)
        BN_EPS = 1e-05
        key = jax.random.key(seed)
        ks = jax.random.split(key, 10)
        feature = jax.random.normal(ks[0], (N, D), dtype=jnp.float32)
        src = jax.random.randint(ks[1], (E,), 0, N, dtype=jnp.int32)
        dst = jax.random.randint(ks[2], (E,), 0, N, dtype=jnp.int32)
        W1 = jax.random.normal(ks[3], (D, D), dtype=jnp.float32) / np.sqrt(D)
        b1 = jnp.zeros((D,), dtype=jnp.float32)
        W2 = jax.random.normal(ks[4], (D, D), dtype=jnp.float32) / np.sqrt(D)
        b2 = jnp.zeros((D,), dtype=jnp.float32)
        gamma = jnp.ones((D,), dtype=jnp.float32)
        beta = jnp.zeros((D,), dtype=jnp.float32)
        eps = jnp.zeros((1,), dtype=jnp.float32)
        return {'feature': feature, 'src': src, 'dst': dst, 'W1': W1, 'b1': b1, 'W2': W2, 'b2': b2, 'gamma': gamma, 'beta': beta, 'eps': eps}
    _L1_gnn_all = _L1_gnn_setup()
    _L1_gnn_in = {k: v for k, v in _L1_gnn_all.items() if k in ('W1', 'b1', 'W2', 'b2', 'gamma', 'beta', 'eps')}
    del _L1_gnn_all

    def _L2_gnn_setup():
        import jax, jax.numpy as jnp
        import numpy as np
        N_NODES = 6250
        N_EDGES = 100000
        D = 96
        LN_EPS = 1e-05

        def _layer(h, src, dst, norm, n_nodes, W, b, g, be):
            h = h @ W
            msg = h[src] * norm[:, None]
            h = jax.ops.segment_sum(msg, dst, num_segments=n_nodes) + b
            h = jnp.tanh(h)
            mu = jnp.mean(h, axis=-1, keepdims=True)
            var = jnp.mean(jnp.square(h - mu), axis=-1, keepdims=True)
            h = (h - mu) * jax.lax.rsqrt(var + LN_EPS)
            return h * g + be
        key = jax.random.key(seed)
        ks = jax.random.split(key, 4)
        x = jax.random.normal(ks[0], (N_NODES, D), dtype=jnp.float32)
        edge_index = jax.random.randint(ks[1], (2, N_EDGES), 0, N_NODES, dtype=jnp.int64)
        scale = 1.0 / np.sqrt(D)
        W0 = jax.random.normal(ks[2], (D, D), dtype=jnp.float32) * scale
        W1 = jax.random.normal(ks[3], (D, D), dtype=jnp.float32) * scale
        b0 = jnp.zeros((D,), jnp.float32)
        b1 = jnp.zeros((D,), jnp.float32)
        g0 = jnp.ones((D,), jnp.float32)
        g1 = jnp.ones((D,), jnp.float32)
        be0 = jnp.zeros((D,), jnp.float32)
        be1 = jnp.zeros((D,), jnp.float32)
        return {'x': x, 'edge_index': edge_index, 'W0': W0, 'b0': b0, 'g0': g0, 'be0': be0, 'W1': W1, 'b1': b1, 'g1': g1, 'be1': be1}
    _L2_gnn_all = _L2_gnn_setup()
    _L2_gnn_in = {k: v for k, v in _L2_gnn_all.items() if k in ('W0', 'b0', 'g0', 'be0', 'W1', 'b1', 'g1', 'be1')}
    del _L2_gnn_all

    def _L3_gnn_setup():
        import jax, jax.numpy as jnp
        import numpy as np
        N, E = (6250, 100000)
        DIN = DOUT = 96
        DE = 32

        def _egnn_conv(x, src, dst, edge_attr, W_msg, W_edge, W_root, b):
            msg = x[src] @ W_msg + edge_attr @ W_edge
            agg = jax.ops.segment_max(msg, dst, num_segments=x.shape[0])
            agg = jnp.where(jnp.isneginf(agg), 0.0, agg)
            return agg + x @ W_root + b
        key = jax.random.key(seed)
        ks = jax.random.split(key, 10)
        rn = lambda k, sh, sc: jax.random.normal(k, sh, jnp.float32) * sc
        return {'X': rn(ks[0], (N, DIN), 1.0), 'edge_index': jax.random.randint(ks[1], (2, E), 0, N, jnp.int32), 'edge_attr': rn(ks[2], (E, DE), 1.0), 'W1_msg': rn(ks[3], (DIN, DOUT), DIN ** (-0.5)), 'W1_edge': rn(ks[4], (DE, DOUT), DE ** (-0.5)), 'W1_root': rn(ks[5], (DIN, DOUT), DIN ** (-0.5)), 'b1': jnp.zeros((DOUT,), jnp.float32), 'W2_msg': rn(ks[6], (DOUT, DOUT), DOUT ** (-0.5)), 'W2_edge': rn(ks[7], (DE, DOUT), DE ** (-0.5)), 'W2_root': rn(ks[8], (DOUT, DOUT), DOUT ** (-0.5)), 'b2': jnp.zeros((DOUT,), jnp.float32)}
    _L3_gnn_all = _L3_gnn_setup()
    _L3_gnn_in = {k: v for k, v in _L3_gnn_all.items() if k in ('W1_msg', 'W1_edge', 'W1_root', 'b1', 'W2_msg', 'W2_edge', 'W2_root', 'b2')}
    del _L3_gnn_all
    return {'x': x, 'src': src, 'dst': dst, 'edge_attr_32': edge_attr_32, 'L0_gnn_W1': _L0_gnn_in['W1'], 'L0_gnn_b1': _L0_gnn_in['b1'], 'L0_gnn_W2': _L0_gnn_in['W2'], 'L0_gnn_b2': _L0_gnn_in['b2'], 'L0_gnn_ln_in_w': _L0_gnn_in['ln_in_w'], 'L0_gnn_ln_in_b': _L0_gnn_in['ln_in_b'], 'L0_gnn_ln_out_w': _L0_gnn_in['ln_out_w'], 'L0_gnn_ln_out_b': _L0_gnn_in['ln_out_b'], 'L1_gnn_W1': _L1_gnn_in['W1'], 'L1_gnn_b1': _L1_gnn_in['b1'], 'L1_gnn_W2': _L1_gnn_in['W2'], 'L1_gnn_b2': _L1_gnn_in['b2'], 'L1_gnn_gamma': _L1_gnn_in['gamma'], 'L1_gnn_beta': _L1_gnn_in['beta'], 'L1_gnn_eps': _L1_gnn_in['eps'], 'L2_gnn_W0': _L2_gnn_in['W0'], 'L2_gnn_b0': _L2_gnn_in['b0'], 'L2_gnn_g0': _L2_gnn_in['g0'], 'L2_gnn_be0': _L2_gnn_in['be0'], 'L2_gnn_W1': _L2_gnn_in['W1'], 'L2_gnn_b1': _L2_gnn_in['b1'], 'L2_gnn_g1': _L2_gnn_in['g1'], 'L2_gnn_be1': _L2_gnn_in['be1'], 'L3_gnn_W1_msg': _L3_gnn_in['W1_msg'], 'L3_gnn_W1_edge': _L3_gnn_in['W1_edge'], 'L3_gnn_W1_root': _L3_gnn_in['W1_root'], 'L3_gnn_b1': _L3_gnn_in['b1'], 'L3_gnn_W2_msg': _L3_gnn_in['W2_msg'], 'L3_gnn_W2_edge': _L3_gnn_in['W2_edge'], 'L3_gnn_W2_root': _L3_gnn_in['W2_root'], 'L3_gnn_b2': _L3_gnn_in['b2']}

def reference(x, src, dst, edge_attr_32, L0_gnn_W1, L0_gnn_b1, L0_gnn_W2, L0_gnn_b2, L0_gnn_ln_in_w, L0_gnn_ln_in_b, L0_gnn_ln_out_w, L0_gnn_ln_out_b, L1_gnn_W1, L1_gnn_b1, L1_gnn_W2, L1_gnn_b2, L1_gnn_gamma, L1_gnn_beta, L1_gnn_eps, L2_gnn_W0, L2_gnn_b0, L2_gnn_g0, L2_gnn_be0, L2_gnn_W1, L2_gnn_b1, L2_gnn_g1, L2_gnn_be1, L3_gnn_W1_msg, L3_gnn_W1_edge, L3_gnn_W1_root, L3_gnn_b1, L3_gnn_W2_msg, L3_gnn_W2_edge, L3_gnn_W2_root, L3_gnn_b2):
    import jax
    import jax.numpy as jnp

    def _L0_gnn_ref(x, edge_index, W1, b1, W2, b2, ln_in_w, ln_in_b, ln_out_w, ln_out_b):
        import jax, jax.numpy as jnp
        import numpy as np
        N = 6250
        E = 100000
        D = 96
        EPS = 1e-05

        def layer_norm(x, w, b):
            mu = jnp.mean(x, axis=-1, keepdims=True)
            var = jnp.var(x, axis=-1, keepdims=True)
            return (x - mu) / jnp.sqrt(var + EPS) * w + b

        def gcn_conv(x, W, b, row, col, n):
            h = x @ W
            loops = jnp.arange(n, dtype=row.dtype)
            row2 = jnp.concatenate([row, loops])
            col2 = jnp.concatenate([col, loops])
            deg = jax.ops.segment_sum(jnp.ones(row2.shape[0], dtype=h.dtype), col2, num_segments=n)
            dinv = jnp.where(deg > 0, deg ** (-0.5), 0.0)
            norm = dinv[row2] * dinv[col2]
            out = jax.ops.segment_sum(h[row2] * norm[:, None], col2, num_segments=n)
            return out + b
        row, col = (edge_index[0], edge_index[1])
        n = x.shape[0]
        y = layer_norm(x, ln_in_w, ln_in_b)
        y = jax.nn.relu(gcn_conv(y, W1, b1, row, col, n))
        y = gcn_conv(y, W2, b2, row, col, n)
        y = layer_norm(y, ln_out_w, ln_out_b)
        return y

    def _L1_gnn_ref(feature, src, dst, W1, b1, W2, b2, gamma, beta, eps):
        import jax, jax.numpy as jnp
        import numpy as np
        N, E, D = (6250, 100000, 96)
        BN_EPS = 1e-05
        n_nodes = feature.shape[0]
        pooled = jax.ops.segment_sum(feature[src], dst, num_segments=n_nodes)
        pooled = pooled + (1.0 + eps[0]) * feature
        h = jax.nn.relu(pooled @ W1 + b1) @ W2 + b2
        mean = jnp.mean(h, axis=0)
        var = jnp.var(h, axis=0)
        h = (h - mean) * jax.lax.rsqrt(var + BN_EPS) * gamma + beta
        return jax.nn.relu(h)

    def _L2_gnn_ref(x, edge_index, W0, b0, g0, be0, W1, b1, g1, be1):
        import jax, jax.numpy as jnp
        import numpy as np
        N_NODES = 6250
        N_EDGES = 100000
        D = 96
        LN_EPS = 1e-05

        def _layer(h, src, dst, norm, n_nodes, W, b, g, be):
            h = h @ W
            msg = h[src] * norm[:, None]
            h = jax.ops.segment_sum(msg, dst, num_segments=n_nodes) + b
            h = jnp.tanh(h)
            mu = jnp.mean(h, axis=-1, keepdims=True)
            var = jnp.mean(jnp.square(h - mu), axis=-1, keepdims=True)
            h = (h - mu) * jax.lax.rsqrt(var + LN_EPS)
            return h * g + be
        n = x.shape[0]
        loops = jnp.arange(n, dtype=edge_index.dtype)
        src = jnp.concatenate([edge_index[0], loops])
        dst = jnp.concatenate([edge_index[1], loops])
        deg = jax.ops.segment_sum(jnp.ones(src.shape, x.dtype), dst, num_segments=n)
        dis = jax.lax.rsqrt(deg)
        norm = dis[src] * dis[dst]
        h = _layer(x, src, dst, norm, n, W0, b0, g0, be0)
        h = _layer(h, src, dst, norm, n, W1, b1, g1, be1)
        return h

    def _L3_gnn_ref(X, edge_index, edge_attr, W1_msg, W1_edge, W1_root, b1, W2_msg, W2_edge, W2_root, b2):
        import jax, jax.numpy as jnp
        import numpy as np
        N, E = (6250, 100000)
        DIN = DOUT = 96
        DE = 32

        def _egnn_conv(x, src, dst, edge_attr, W_msg, W_edge, W_root, b):
            msg = x[src] @ W_msg + edge_attr @ W_edge
            agg = jax.ops.segment_max(msg, dst, num_segments=x.shape[0])
            agg = jnp.where(jnp.isneginf(agg), 0.0, agg)
            return agg + x @ W_root + b
        src, dst = (edge_index[0], edge_index[1])
        c1 = jax.nn.leaky_relu(_egnn_conv(X, src, dst, edge_attr, W1_msg, W1_edge, W1_root, b1))
        c2 = jax.nn.leaky_relu(_egnn_conv(c1, src, dst, edge_attr, W2_msg, W2_edge, W2_root, b2))
        return c2
    edge_index = jnp.stack([src, dst])
    h = jnp.maximum(_layernorm(x, axis=-1), 0.0)
    x = x + _L0_gnn_ref(h, edge_index, L0_gnn_W1, L0_gnn_b1, L0_gnn_W2, L0_gnn_b2, L0_gnn_ln_in_w, L0_gnn_ln_in_b, L0_gnn_ln_out_w, L0_gnn_ln_out_b)
    h = jnp.maximum(_layernorm(x, axis=-1), 0.0)
    x = x + _L1_gnn_ref(h, src, dst, L1_gnn_W1, L1_gnn_b1, L1_gnn_W2, L1_gnn_b2, L1_gnn_gamma, L1_gnn_beta, L1_gnn_eps)
    h = jnp.maximum(_layernorm(x, axis=-1), 0.0)
    x = x + _L2_gnn_ref(h, edge_index, L2_gnn_W0, L2_gnn_b0, L2_gnn_g0, L2_gnn_be0, L2_gnn_W1, L2_gnn_b1, L2_gnn_g1, L2_gnn_be1)
    h = jnp.maximum(_layernorm(x, axis=-1), 0.0)
    x = x + _L3_gnn_ref(h, edge_index, edge_attr_32, L3_gnn_W1_msg, L3_gnn_W1_edge, L3_gnn_W1_root, L3_gnn_b1, L3_gnn_W2_msg, L3_gnn_W2_edge, L3_gnn_W2_root, L3_gnn_b2)
    return x

_drawn_inputs = setup_inputs


def setup_inputs(seed=0):
    import zlib

    import numpy as np

    out = dict(_drawn_inputs(seed))
    spreads = {'L0_gnn_b1': (0.0, 0.1),
     'L0_gnn_b2': (0.0, 0.1),
     'L0_gnn_ln_in_w': (1.0, 0.6),
     'L0_gnn_ln_in_b': (0.0, 0.1),
     'L0_gnn_ln_out_w': (1.0, 0.2),
     'L0_gnn_ln_out_b': (0.0, 0.1),
     'L1_gnn_b1': (0.0, 2.0),
     'L1_gnn_b2': (0.0, 2.0),
     'L1_gnn_gamma': (1.0, 0.2),
     'L1_gnn_beta': (0.0, 0.395),
     'L2_gnn_b0': (0.0, 0.1),
     'L2_gnn_g0': (1.0, 0.546),
     'L2_gnn_be0': (0.0, 0.282),
     'L2_gnn_b1': (0.0, 0.37),
     'L2_gnn_g1': (1.0, 0.2),
     'L2_gnn_be1': (0.0, 0.333),
     'L3_gnn_b1': (0.0, 0.272),
     'L3_gnn_b2': (0.0, 0.477)}
    factors = {}
    for name, (base, spread) in spreads.items():
        noise = np.random.default_rng([zlib.crc32(name.encode()), seed]).standard_normal(out[name].shape)
        drawn = base * np.exp(spread * noise) if base else spread * noise
        out[name] = jnp.asarray(drawn.astype(out[name].dtype))
    for name, factor in factors.items():
        out[name] = (out[name] * factor).astype(out[name].dtype)
    return out
```

```python
from contextlib import ExitStack

import concourse.bass as bass
from concourse import mybir

P = 128
N = 6250
E = 200000
D = 96
DE = 32
NT = (N + P - 1) // P
GT = 4
NG = (NT + GT - 1) // GT
TT = NG * GT
TAIL = N - (NT - 1) * P
QUAD = 4 * P
CH = 16
HALF = CH * P
BODIES = (E + 2 * HALF - 1) // (2 * HALF)
HALVES = 2 * BODIES
EP = HALVES * HALF
SLOTS = 8
EPS = 1e-5
NEG = -3.38e38
SUM, MAX = 0, 1

ALU = mybir.AluOpType
ACT = mybir.ActivationFunctionType
AX = mybir.AxisListType
F32 = mybir.dt.float32
BF16 = mybir.dt.bfloat16
I32 = mybir.dt.int32
U32 = mybir.dt.uint32

ROWS = ["L0_gnn_ln_in_w", "L0_gnn_ln_in_b", "L0_gnn_b1", "L0_gnn_b2", "L0_gnn_ln_out_w", "L0_gnn_ln_out_b",
        "L1_gnn_b1", "L1_gnn_b2", "L1_gnn_gamma", "L1_gnn_beta", "L2_gnn_b0", "L2_gnn_g0", "L2_gnn_be0",
        "L2_gnn_b1", "L2_gnn_g1", "L2_gnn_be1", "L3_gnn_b1", "L3_gnn_b2"]
MATS = ["L0_gnn_W1", "L0_gnn_W2", "L1_gnn_W1", "L1_gnn_W2", "L2_gnn_W0", "L2_gnn_W1", "L3_gnn_W1_msg",
        "L3_gnn_W1_root", "L3_gnn_W2_msg", "L3_gnn_W2_root"]
EDGE_MATS = ["L3_gnn_W1_edge", "L3_gnn_W2_edge"]
KINDS = [SUM, SUM, SUM, SUM, SUM, MAX, MAX]


def gnn_program(nc, a, out):
    with ExitStack() as ctx:
        def sb(name, shape, dt=F32):
            return ctx.enter_context(nc.sbuf_tensor(name, shape, dt))

        def ps(name, shape, dt=F32):
            return ctx.enter_context(nc.psum_tensor(name, shape, dt))

        def sem(name):
            return ctx.enter_context(nc.semaphore(name))

        table_d = nc.dram_tensor("table_scratch", (NT * P, D), F32, kind="Internal").ap()
        scan_d = nc.dram_tensor("scan_scratch", (EP, D), F32, kind="Internal").ap()
        flag_d = [nc.dram_tensor(f"flag_scratch_{n}", (HALVES, HALF), BF16, kind="Internal").ap()
                  for n in ("sum", "max")]

        X = sb("X", [P, TT, D])
        H = sb("H", [P, TT, D])
        U = sb("U", [P, TT, D])
        V = sb("V", [P, TT, D])
        Z = sb("Z", [P, TT, D])
        rows = sb("rows", [P, len(ROWS), D])
        mats = sb("mats", [D, len(MATS), D])
        emats = sb("emats", [DE, 2, D])
        gin_eps = sb("gin_eps", [P, 1])
        iota_i = sb("iota_i", [P, P], I32)
        part_i = sb("part_i", [P, 1], I32)
        iota_f = sb("iota_f", [P, P])
        iota_b = sb("iota_b", [P, P], BF16)
        part_f = sb("part_f", [P, 1])
        ident = sb("ident", [P, P])
        upper = sb("upper", [P, P])
        ones = sb("ones", [P, P])
        real_row = sb("real_row", [P, 1])
        zero_b = sb("zero_b", [P, P], BF16)
        count = sb("count", [P, TT])
        upto = sb("upto", [P, TT])
        colsum = sb("colsum", [P, TT])
        has_edge = sb("has_edge", [P, TT])
        dinv = sb("dinv", [P, TT])
        last_row = sb("last_row", [P, TT], U32)
        last_a = sb("last_a", [P, TT], I32)
        last_b = sb("last_b", [P, TT], I32)
        mean = sb("mean", [P, TT])
        rstd = sb("rstd", [P, TT])
        bn_a = sb("bn_a", [P, D])
        bn_b = sb("bn_b", [P, D])
        bn_c = sb("bn_c", [P, D])
        idx = sb("idx", [P, 2, CH], U32)
        keep = sb("keep", [D, 2, HALF], BF16)
        ea = sb("ea", [DE, 2, HALF])
        ring = sb("ring", [P, SLOTS * 4, D])
        scan = sb("scan", [D, 2, QUAD])
        stored = sb("stored", [P, 2, CH, D])
        stage = sb("stage", [P, GT, D])
        yT = sb("yT", [D, GT * P])
        dst_i = H[:, :, :].rearrange("p t d -> p (t d)").bitcast(I32)[:, 0:HALVES * CH]
        lo_i = H[:, :, :].rearrange("p t d -> p (t d)").bitcast(I32)[:, HALVES * CH:2 * HALVES * CH]
        lo_f = U[:, :, :].rearrange("p t d -> p (t d)")[:, 0:HALVES * CH]
        hi_f = U[:, :, :].rearrange("p t d -> p (t d)")[:, HALVES * CH:2 * HALVES * CH]
        cur_i = V[:, :, :].rearrange("p t d -> p (t d)").bitcast(I32)[0:HALVES, 0:HALF]
        prev_i = V[:, :, :].rearrange("p t d -> p (t d)").bitcast(I32)[0:HALVES, HALF:2 * HALF]
        same = Z[:, :, :].rearrange("p t d -> p (t d)")[0:HALVES, 0:HALF].bitcast(BF16)[:, 0:HALF]
        newseg = Z[:, :, :].rearrange("p t d -> p (t d)")[0:HALVES, HALF:2 * HALF].bitcast(BF16)[:, 0:HALF]
        hot_lo = ring[:, :, :].rearrange("p c d -> p (c d)").bitcast(BF16)[:, 0:2 * CH * P].rearrange(
            "p (h c m) -> p h c m", h=2, c=CH)
        hot_hi = stored[:, :, :, :].rearrange("p h c d -> p h (c d)").bitcast(BF16)[:, :, 0:CH * 64].rearrange(
            "p h (c m) -> p h c m", m=64)

        psF = [ps(f"psF{i}", [P, QUAD]) for i in range(2)]
        psB = [ps(f"psB{i}", [P, QUAD]) for i in range(2)]
        psT = ps("psT", [P, QUAD])
        psM = ps("psM", [P, QUAD])
        psX = ps("psX", [P, QUAD])

        s_param = sem("params_loaded")
        s_x = sem("x_loaded")
        s_dst = sem("dst_loaded")
        s_prev = sem("prev_loaded")
        s_iota = sem("iota_made")
        s_const = sem("consts_made")
        s_flag = sem("flags_made")
        s_flagw = sem("flags_written")
        s_lohi = sem("lo_hi_made")
        s_hot = sem("one_hots_made")
        s_hotu = sem("one_hots_used")
        s_hist = sem("histogram_done")
        s_cnt = sem("count_copied")
        s_pre = sem("prefix_done")
        s_v = sem("vector_chain")
        s_to_act = sem("vector_to_scalar")
        s_from_act = sem("scalar_to_vector")
        s_to_pe = sem("vector_to_tensor")
        s_from_pe = sem("tensor_to_vector")
        s_tbl = sem("table_ready")
        s_tblw = sem("table_written")
        s_idx = [sem(f"idx_landed_{h}") for h in range(2)]
        s_keep = [sem(f"keep_landed_{h}") for h in range(2)]
        s_ea = [sem(f"edge_attr_landed_{h}") for h in range(2)]
        s_g = [sem(f"gathered_{s}") for s in range(SLOTS)]
        s_turn = sem("gather_turns")
        s_fwd = sem("feature_major_done")
        s_scan = sem("scan_done")
        s_back = sem("edge_major_done")
        s_evac = sem("edge_major_copied")
        s_st = [sem(f"scan_stored_{h}") for h in range(2)]
        s_agg = sem("aggregates_landed")
        s_lin = sem("linear_input_ready")
        s_stage = sem("linear_staged")
        s_lt = sem("linear_transposed")
        s_yt = sem("linear_transpose_copied")
        s_lm = sem("linear_product_done")
        s_lo = sem("linear_product_copied")
        s_outr = sem("output_ready")
        s_out = sem("output_stored")

        def node(t):
            return t[:, 0:NT, :]

        def per_node(t):
            return t[:, 0:NT].unsqueeze(2).to_broadcast([P, NT, D])

        def per_feature(t):
            return t.unsqueeze(1).to_broadcast([P, NT, D])

        def row(name):
            return rows[:, ROWS.index(name), :]

        def mat(name):
            return mats[:, MATS.index(name), :]

        LIN = [(U, "L0_gnn_W1", V), (U, "L0_gnn_W2", V), (U, "L1_gnn_W1", V), (U, "L1_gnn_W2", V),
               (H, "L2_gnn_W0", V), (H, "L2_gnn_W1", V), (H, "L3_gnn_W1_msg", V), (H, "L3_gnn_W1_root", V),
               (H, "L3_gnn_W2_msg", V), (H, "L3_gnn_W2_root", V)]
        STEPS = [("lin", 0), ("conv", 0), ("lin", 1), ("conv", 1), ("conv", 2), ("lin", 2), ("lin", 3),
                 ("lin", 4), ("conv", 3), ("lin", 5), ("conv", 4),
                 ("lin", 6), ("conv", 5), ("lin", 7), ("lin", 8), ("conv", 6), ("lin", 9)]

        block = ctx.enter_context(nc.Block())

        @block.sync
        def _(sp):
            sp.dma_start(dst_i, a["dst_chunks"].rearrange("h p c -> p h c")).then_inc(s_dst, 16)
            sp.dma_start(cur_i, a["dst_line"].rearrange("(h e) -> h e", e=HALF)).then_inc(s_prev, 16)
            sp.wait_ge(s_v, 2)
            sp.dma_start(prev_i[0:1, 1:HALF], a["dst_line"][0:HALF - 1].unsqueeze(0)).then_inc(s_prev, 16)
            sp.dma_start(prev_i[1:HALVES, :], a["dst_line"][HALF - 1:EP - 1].rearrange("(h e) -> h e", e=HALF)
                         ).then_inc(s_prev, 16)
            sp.dma_start(X[:, 0:NT - 1, :], a["x"][0:(NT - 1) * P, :].rearrange("(t p) d -> p t d", p=P)
                         ).then_inc(s_x, 16)
            sp.dma_start(X[0:TAIL, NT - 1, :], a["x"][(NT - 1) * P:N, :]).then_inc(s_x, 16)
            for i, name in enumerate(ROWS):
                sp.dma_start(rows[:, i, :], a[name].partition_broadcast(P)).then_inc(s_param, 16)
            for i, name in enumerate(MATS):
                sp.dma_start(mats[:, i, :], a[name]).then_inc(s_param, 16)
            for i, name in enumerate(EDGE_MATS):
                sp.dma_start(emats[:, i, :], a[name]).then_inc(s_param, 16)
            sp.dma_start(gin_eps[:, :], a["L1_gnn_eps"].partition_broadcast(P)).then_inc(s_param, 16)
            sp.wait_ge(s_flag, 1)
            sp.dma_start(flag_d[SUM], same).then_inc(s_flagw, 16)
            sp.dma_start(flag_d[MAX], newseg).then_inc(s_flagw, 16)
            sp.wait_ge(s_flagw, 32)

            def conv_loads(k):
                kind = KINDS[k]
                sp.wait_ge(s_tbl, k + 1)
                sp.dma_start(table_d.rearrange("(t p) d -> p t d", p=P), node(H if k == 2 else V)
                             ).then_inc(s_tblw, 16)
                with sp.Fori(0, BODIES) as it:
                    for h in range(2):
                        half = sp.snap(it * 2 + h)
                        sp.wait_ge(s_fwd, it * 8 + (8 * BODIES * k + 4 * h + 4))
                        sp.wait_ge(s_scan, it * 8 + (8 * BODIES * k + 4 * h + 4))
                        sp.sem_inc(s_turn, 1)
                        sp.dma_start(idx[:, h, :], a["src_chunks"][bass.ds(half, 1), :, :].rearrange("a p c -> p (a c)")
                                     ).then_inc(s_idx[h], 16)
                        sp.dma_start(keep[:, h, :], flag_d[kind][bass.ds(half, 1), :].rearrange("a e -> (a e)")
                                     .partition_broadcast(D)).then_inc(s_keep[h], 16)
                        if kind == MAX:
                            sp.dma_start(ea[:, h, :], a["edge_attr_halves"][bass.ds(half, 1), :, :].rearrange(
                                "a f e -> f (a e)")).then_inc(s_ea[h], 16)

            for k in range(len(KINDS)):
                conv_loads(k)
            sp.wait_ge(s_outr, 1)
            sp.dma_start(out[0:(NT - 1) * P, :].rearrange("(t p) d -> p t d", p=P), X[:, 0:NT - 1, :]
                         ).then_inc(s_out, 16)
            sp.dma_start(out[(NT - 1) * P:N, :], X[0:TAIL, NT - 1, :]).then_inc(s_out, 16)
            sp.wait_ge(s_out, 32)

        @block.gpsimd
        def _(pool):
            nc.gpsimd.iota(iota_i[:, :], pattern=[[1, P]], base=0, channel_multiplier=0).then_inc(s_iota, 1)
            nc.gpsimd.iota(part_i[:, :], pattern=[[0, 1]], base=0, channel_multiplier=1).then_inc(s_iota, 1)
            for k in range(len(KINDS)):
                pool.wait_ge(s_tblw, 16 * (k + 1))
                with pool.Fori(0, BODIES) as it:
                    for h in range(2):
                        pool.wait_ge(s_idx[h], it * 16 + (16 * BODIES * k + 16))
                        pool.wait_ge(s_fwd, it * 8 + (8 * BODIES * k + 4 * h + 4))
                        pool.sem_inc(s_turn, 1)
                        for c in range(CH):
                            nc.gpsimd.indirect_dma_start(
                                ring[:, h * CH + c, :], None, table_d,
                                bass.IndirectOffsetOnAxis(ap=idx[:, h, c:c + 1], axis=0)
                            ).then_inc(s_g[4 * h + c // 4], 16)
                pool.wait_ge(s_st[0], 16 * (BODIES * (k + 1) + 1))
                pool.wait_ge(s_st[1], 16 * (BODIES * (k + 1) + 1))
                for t in range(NT):
                    nc.gpsimd.indirect_dma_start(
                        Z[:, t, :], None, scan_d, bass.IndirectOffsetOnAxis(ap=last_row[:, t:t + 1], axis=0)
                    ).then_inc(s_agg, 16)

        @block.tensor
        def _(pe):
            pe.sem_inc(s_fwd, 8)
            pe.sem_inc(s_back, 2)
            pe.sem_inc(s_hotu, 2)
            pe.sem_inc(s_lt, 1)
            pe.sem_inc(s_lm, 1)
            pe.wait_ge(s_const, 1)
            hist = psX[:, 0:64]
            nc.tensor.matmul(hist, zero_b[:, :], zero_b[:, 0:64], start=True, stop=False)
            with pe.Fori(0, BODIES) as it:
                for h in range(2):
                    pe.wait_ge(s_hot, it * 2 + (h + 1))
                    for c in range(CH):
                        last = nc.tensor.matmul(hist, hot_lo[:, h, c, :], hot_hi[:, h, c, :], start=False, stop=False)
                    last.then_inc(s_hotu, 1)
            nc.tensor.matmul(hist, zero_b[:, :], zero_b[:, 0:64], start=False, stop=True).then_inc(s_hist, 1)
            pe.wait_ge(s_cnt, 1)
            nc.tensor.matmul(psT[:, 0:TT], upper[:, :], count[:, :], start=True, stop=True)
            nc.tensor.matmul(psM[:, 0:TT], ones[:, :], count[:, :], start=True, stop=True).then_inc(s_pre, 1)

            def linear(j):
                src, w, dst = LIN[j]
                with pe.Fori(0, NG) as g:
                    pe.wait_ge(s_stage, g + (NG * j + 1))
                    pe.wait_ge(s_yt, g + (NG * j + 1))
                    for t in range(GT):
                        last = nc.tensor.transpose(psT[0:D, t * P:(t + 1) * P], stage[:, t, :], ident[:, :])
                    last.then_inc(s_lt, 1)
                    pe.wait_ge(s_yt, g + (NG * j + 2))
                    pe.wait_ge(s_lo, g + (NG * j + 1))
                    for t in range(GT):
                        last = nc.tensor.matmul(psM[:, t * D:(t + 1) * D], yT[:, t * P:(t + 1) * P], mat(w),
                                                start=True, stop=True)
                    last.then_inc(s_lm, 1)

            def conv(k):
                base = 8 * BODIES * k

                def feature_major(it, s):
                    h, q, b = s // 4, s % 4, s % 2
                    pe.wait_ge(s_scan, it * 8 + (base + s + 7))
                    pe.wait_ge(s_g[s], it * 64 + (64 * BODIES * k + 64))
                    if KINDS[k] == MAX:
                        pe.wait_ge(s_ea[h], it * 16 + (16 * BODIES * (k - 5) + 16))
                        nc.tensor.matmul(psF[b][0:D, :], emats[:, k - 5, :], ea[:, h, q * QUAD:(q + 1) * QUAD],
                                         start=True, stop=False)
                    for c in range(4):
                        rows_in = ring[:, 4 * s + c, :]
                        if KINDS[k] == MAX:
                            last = nc.tensor.matmul(psF[b][0:D, c * P:(c + 1) * P], rows_in, ident[:, :],
                                                    start=False, stop=(c == 3))
                        else:
                            last = nc.tensor.transpose(psF[b][0:D, c * P:(c + 1) * P], rows_in, ident[:, :])
                    last.then_inc(s_fwd, 1)

                def edge_major(it, s):
                    b = s % 2
                    pe.wait_ge(s_scan, it * 8 + (base + s + 9))
                    pe.wait_ge(s_evac, it * 8 + (base + s + 1))
                    for c in range(4):
                        last = nc.tensor.transpose(psB[b][:, c * D:(c + 1) * D], scan[:, b, c * P:(c + 1) * P],
                                                   ident[0:D, 0:D])
                    last.then_inc(s_back, 1)

                with pe.Fori(0, BODIES) as it:
                    feature_major(it, 0)
                    for s in range(SLOTS):
                        if s + 1 < SLOTS:
                            feature_major(it, s + 1)
                        edge_major(it, s)

            pe.wait_ge(s_param, 16 * (len(ROWS) + len(MATS) + len(EDGE_MATS) + 1))
            for what, n in STEPS:
                if what == "lin":
                    linear(n)
                else:
                    conv(n)
                if (what, n) == ("lin", 3):
                    for i in range(2):
                        pe.wait_ge(s_to_pe, i + 1)
                        nc.tensor.matmul(psX[:, i * D:(i + 1) * D], ones[:, :], bn_a[:, :], start=True, stop=True
                                         ).then_inc(s_from_pe, 1)

        @block.scalar
        def _(act):
            act.sem_inc(s_evac, 2)
            act.sem_inc(s_lo, 1)
            act.sem_inc(s_st[0], 16)
            act.sem_inc(s_st[1], 16)
            handed = [0]

            def from_vector(call):
                handed[0] += 1
                act.wait_ge(s_to_act, handed[0])
                call().then_inc(s_from_act, 1)

            def square_and_root():
                from_vector(lambda: nc.scalar.activation(node(Z), node(Z), ACT.Square))
                from_vector(lambda: nc.scalar.activation(rstd[:, 0:NT], rstd[:, 0:NT], ACT.Sqrt))

            def linear(j):
                src, w, dst = LIN[j]
                act.wait_ge(s_lin, j + 1)
                with act.Fori(0, NG) as g:
                    act.wait_ge(s_lt, g + (NG * j + 1))
                    nc.scalar.copy(stage[:, :, :], src[:, bass.ds(g * GT, GT), :]).then_inc(s_stage, 1)
                    act.wait_ge(s_lm, g + (NG * j + 2))
                    nc.scalar.copy(dst[:, bass.ds(g * GT, GT), :],
                                   psM[:, 0:GT * D].rearrange("p (t d) -> p t d", d=D)).then_inc(s_lo, 1)

            def conv(k):
                base = 8 * BODIES * k
                with act.Fori(0, BODIES) as it:
                    for s in range(SLOTS):
                        h, q, b = s // 4, s % 4, s % 2
                        if q == 0:
                            act.wait_ge(s_st[h], it * 16 + (16 * BODIES * k + 16))
                        act.wait_ge(s_back, it * 8 + (base + s + 3))
                        nc.scalar.copy(stored[:, h, q * 4:(q + 1) * 4, :],
                                       psB[b][:, 0:4 * D].rearrange("p (c d) -> p c d", d=D)).then_inc(s_evac, 1)
                        if q == 3:
                            act.wait_ge(s_evac, it * 8 + (base + s + 3))
                            act.dma_start(
                                scan_d.rearrange("(i p c) d -> i p (c d)", p=P, c=CH)[bass.ds(it * 2 + h, 1), :, :]
                                .rearrange("a p m -> p (a m)"),
                                stored[:, h, :, :].rearrange("p c d -> p (c d)")).then_inc(s_st[h], 16)

            from_vector(lambda: nc.scalar.activation(dinv[:, 0:NT], dinv[:, 0:NT], ACT.Sqrt))
            square_and_root()
            square_and_root()
            linear(0)
            conv(0)
            linear(1)
            conv(1)
            square_and_root()
            square_and_root()
            conv(2)
            linear(2)
            linear(3)
            from_vector(lambda: nc.scalar.activation(node(Z), node(Z), ACT.Square))
            from_vector(lambda: nc.scalar.activation(bn_b[:, :], bn_b[:, :], ACT.Sqrt))
            square_and_root()
            linear(4)
            conv(3)
            from_vector(lambda: nc.scalar.activation(node(U), node(U), ACT.Tanh))
            square_and_root()
            linear(5)
            conv(4)
            from_vector(lambda: nc.scalar.activation(node(U), node(U), ACT.Tanh))
            square_and_root()
            square_and_root()
            linear(6)
            conv(5)
            linear(7)
            linear(8)
            conv(6)
            linear(9)

        @block.vector
        def _(dve):
            chained, handed, to_pe = [0], [0], [0]
            V_ = nc.vector

            def link(ins):
                chained[0] += 1
                ins.then_inc(s_v, 1)
                dve.wait_ge(s_v, chained[0])

            def scalar_turn():
                handed[0] += 1
                dve.sem_inc(s_to_act, 1)
                dve.wait_ge(s_from_act, handed[0])

            link(V_.memset(prev_i[0:1, 0:1], -1))
            link(V_.memset(X[:, :, :], 0.0))
            dve.sem_inc(s_scan, 8)
            dve.sem_inc(s_yt, 1)
            V_.memset(scan[:, :, :], 0.0)
            V_.memset(zero_b[:, :], 0.0)
            V_.memset(ones[:, :], 1.0)
            dve.wait_ge(s_iota, 2)
            V_.tensor_copy(iota_f[:, :], iota_i[:, :])
            V_.tensor_copy(iota_b[:, :], iota_i[:, :])
            link(V_.tensor_copy(part_f[:, :], part_i[:, :]))
            V_.tensor_scalar(ident[:, :], iota_f[:, :], part_f[:, 0:1], None, ALU.is_equal)
            V_.tensor_scalar(upper[:, :], iota_f[:, :], part_f[:, 0:1], None, ALU.is_ge)
            V_.tensor_scalar(real_row[:, :], part_f[:, :], float(TAIL), None, ALU.is_lt)
            V_.memset(hot_hi, 0.0).then_inc(s_const, 1)
            dve.wait_ge(s_prev, 48)
            link(V_.tensor_tensor(same, cur_i, prev_i, ALU.is_equal))
            V_.tensor_scalar(newseg, same, -NEG, NEG, ALU.mult, ALU.add).then_inc(s_flag, 1)
            dve.wait_ge(s_dst, 16)
            link(V_.tensor_scalar(lo_i, dst_i, P - 1, None, ALU.bitwise_and))
            link(V_.tensor_copy(lo_f, lo_i))
            link(V_.tensor_scalar(lo_i, dst_i, 7, None, ALU.logical_shift_right))
            link(V_.tensor_copy(hi_f, lo_i))
            with dve.Fori(0, BODIES) as it:
                for h in range(2):
                    dve.wait_ge(s_hotu, it * 2 + (h + 1))
                    for c in range(CH):
                        e = it * (2 * CH) + (h * CH + c)
                        V_.tensor_scalar(hot_lo[:, h, c, :], iota_b[:, :], lo_f[:, bass.ds(e, 1)], None, ALU.is_equal)
                        last = V_.tensor_scalar(hot_hi[:, h, c, 0:TT], iota_b[:, 0:TT], hi_f[:, bass.ds(e, 1)], None,
                                                ALU.is_equal)
                    last.then_inc(s_hot, 1)
            dve.wait_ge(s_hist, 1)
            V_.tensor_copy(count[:, :], psX[:, 0:TT]).then_inc(s_cnt, 1)
            dve.wait_ge(s_cnt, 1)
            V_.tensor_scalar(has_edge[:, :], count[:, :], 0.0, None, ALU.is_gt)
            link(V_.tensor_scalar(dinv[:, :], count[:, :], 1.0, None, ALU.add))
            scalar_turn()
            V_.reciprocal(dinv[:, 0:NT], dinv[:, 0:NT])
            dve.wait_ge(s_pre, 1)
            link(V_.tensor_copy(colsum[:, :], psM[:, 0:TT]))
            link(V_.tensor_tensor_scan(upto[:, :], ones[:, 0:TT], colsum[:, :], 0.0, ALU.mult, ALU.add))
            link(V_.tensor_tensor(upto[:, :], upto[:, :], colsum[:, :], ALU.subtract))
            link(V_.tensor_tensor(upto[:, :], upto[:, :], psT[:, 0:TT], ALU.add))
            link(V_.tensor_scalar(upto[:, :], upto[:, :], 1.0, 0.0, ALU.subtract, ALU.max))
            link(V_.tensor_copy(last_a[:, :], upto[:, :]))
            last_u = last_row[:, :].bitcast(I32)
            link(V_.tensor_scalar(last_b[:, :], last_a[:, :], P - 1, 4, ALU.bitwise_and, ALU.logical_shift_left))
            V_.tensor_scalar(last_u, last_a[:, :], 7, CH - 1, ALU.logical_shift_right, ALU.bitwise_and)
            link(V_.tensor_scalar(last_a[:, :], last_a[:, :], 11, 11, ALU.logical_shift_right, ALU.logical_shift_left))
            link(V_.tensor_tensor(last_u, last_u, last_b[:, :], ALU.bitwise_or))
            link(V_.tensor_tensor(last_u, last_u, last_a[:, :], ALU.bitwise_or))
            dve.wait_ge(s_flagw, 32)
            link(V_.memset(H[:, :, :], 0.0))
            link(V_.memset(U[:, :, :], 0.0))
            link(V_.memset(V[:, :, :], 0.0))
            dve.wait_ge(s_x, 32)
            dve.wait_ge(s_param, 16 * (len(ROWS) + len(MATS) + len(EDGE_MATS) + 1))

            def layernorm(dst, src, w=None, b=None, relu=False):
                link(V_.tensor_reduce(mean[:, 0:NT], node(src), AX.X, ALU.add))
                link(V_.tensor_scalar(mean[:, 0:NT], mean[:, 0:NT], 1.0 / D, None, ALU.mult))
                link(V_.tensor_tensor(node(dst), node(src), per_node(mean), ALU.subtract))
                link(V_.tensor_copy(node(Z), node(dst)))
                scalar_turn()
                link(V_.tensor_reduce(rstd[:, 0:NT], node(Z), AX.X, ALU.add))
                link(V_.tensor_scalar(rstd[:, 0:NT], rstd[:, 0:NT], 1.0 / D, EPS, ALU.mult, ALU.add))
                scalar_turn()
                link(V_.reciprocal(rstd[:, 0:NT], rstd[:, 0:NT]))
                link(V_.tensor_tensor(node(dst), node(dst), per_node(rstd), ALU.mult))
                if w is not None:
                    link(V_.tensor_tensor(node(dst), node(dst), per_feature(row(w)), ALU.mult))
                    link(V_.tensor_tensor(node(dst), node(dst), per_feature(row(b)), ALU.add))
                if relu:
                    link(V_.tensor_scalar(node(dst), node(dst), 0.0, None, ALU.max))

            def linear(j):
                dve.sem_inc(s_lin, 1)
                with dve.Fori(0, NG) as g:
                    dve.wait_ge(s_lt, g + (NG * j + 2))
                    dve.wait_ge(s_lm, g + (NG * j + 1))
                    V_.tensor_copy(yT[:, :], psT[0:D, :]).then_inc(s_yt, 1)
                dve.wait_ge(s_lo, NG * (j + 1) + 1)

            def conv(k):
                base = 8 * BODIES * k
                op0, op1 = (ALU.add, ALU.max) if KINDS[k] == MAX else (ALU.mult, ALU.add)
                dve.sem_inc(s_tbl, 1)
                with dve.Fori(0, BODIES) as it:
                    for s in range(SLOTS):
                        h, q, b = s // 4, s % 4, s % 2
                        if q == 0:
                            dve.wait_ge(s_keep[h], it * 16 + (16 * BODIES * k + 16))
                        dve.wait_ge(s_fwd, it * 8 + (base + s + 9))
                        dve.wait_ge(s_back, it * 8 + (base + s + 1))
                        dve.wait_ge(s_scan, it * 8 + (base + s + 8))
                        V_.tensor_tensor_scan(scan[:, b, :], keep[:, h, q * QUAD:(q + 1) * QUAD], psF[b][0:D, :],
                                              scan[:, 1 - b, QUAD - 1:QUAD], op0, op1).then_inc(s_scan, 1)
                dve.wait_ge(s_agg, 16 * NT * (k + 1))
                link(V_.tensor_tensor(node(Z), node(Z), per_node(has_edge), ALU.mult))

            def scale(t):
                link(V_.tensor_tensor(node(t), node(t), per_node(dinv), ALU.mult))

            def add(dst, x, y):
                link(V_.tensor_tensor(node(dst), node(x), node(y), ALU.add))

            def add_row(t, name):
                link(V_.tensor_tensor(node(t), node(t), per_feature(row(name)), ALU.add))

            def gcn(j, k, bias):
                linear(j)
                scale(V)
                conv(k)
                add(U, Z, V)
                scale(U)
                add_row(U, bias)

            layernorm(H, X, relu=True)
            layernorm(U, H, "L0_gnn_ln_in_w", "L0_gnn_ln_in_b")
            gcn(0, 0, "L0_gnn_b1")
            link(V_.tensor_scalar(node(U), node(U), 0.0, None, ALU.max))
            gcn(1, 1, "L0_gnn_b2")
            layernorm(H, U, "L0_gnn_ln_out_w", "L0_gnn_ln_out_b")
            add(X, X, H)
            layernorm(H, X, relu=True)
            conv(2)
            link(V_.tensor_scalar(gin_eps[:, :], gin_eps[:, :], 1.0, None, ALU.add))
            link(V_.scalar_tensor_tensor(node(U), node(H), gin_eps[:, 0:1], node(Z), ALU.mult, ALU.add))
            linear(2)
            link(V_.tensor_tensor(node(U), node(V), per_feature(row("L1_gnn_b1")), ALU.add))
            link(V_.tensor_scalar(node(U), node(U), 0.0, None, ALU.max))
            linear(3)
            add_row(V, "L1_gnn_b2")

            def clear_tail(t):
                link(V_.tensor_scalar(t[:, NT - 1, :], t[:, NT - 1, :], real_row[:, 0:1], None, ALU.mult))

            def feature_sums(t, i):
                link(V_.tensor_reduce(bn_a[:, :], node(t).rearrange("p t d -> p d t"), AX.X, ALU.add))
                dve.sem_inc(s_to_pe, 1)
                dve.wait_ge(s_from_pe, i + 1)

            clear_tail(V)
            feature_sums(V, 0)
            link(V_.tensor_scalar(bn_b[:, :], psX[:, 0:D], 1.0 / N, None, ALU.mult))
            link(V_.tensor_tensor(node(V), node(V), per_feature(bn_b[:, :]), ALU.subtract))
            clear_tail(V)
            link(V_.tensor_copy(node(Z), node(V)))
            scalar_turn()
            feature_sums(Z, 1)
            link(V_.tensor_scalar(bn_b[:, :], psX[:, D:2 * D], 1.0 / N, EPS, ALU.mult, ALU.add))
            scalar_turn()
            link(V_.reciprocal(bn_c[:, :], bn_b[:, :]))
            link(V_.tensor_tensor(bn_c[:, :], bn_c[:, :], row("L1_gnn_gamma"), ALU.mult))
            link(V_.tensor_tensor(node(V), node(V), per_feature(bn_c[:, :]), ALU.mult))
            add_row(V, "L1_gnn_beta")
            link(V_.tensor_scalar(node(V), node(V), 0.0, None, ALU.max))
            add(X, X, V)
            layernorm(H, X, relu=True)
            gcn(4, 3, "L2_gnn_b0")
            scalar_turn()
            layernorm(H, U, "L2_gnn_g0", "L2_gnn_be0")
            gcn(5, 4, "L2_gnn_b1")
            scalar_turn()
            layernorm(H, U, "L2_gnn_g1", "L2_gnn_be1")
            add(X, X, H)
            layernorm(H, X, relu=True)
            for i in range(2):
                linear(6 + 2 * i)
                conv(5 + i)
                linear(7 + 2 * i)
                add(U, Z, V)
                add_row(U, f"L3_gnn_b{i + 1}")
                link(V_.scalar_tensor_tensor(node(H), node(U), 0.01, node(U), ALU.mult, ALU.max))
            V_.tensor_tensor(node(X), node(X), node(H), ALU.add).then_inc(s_outr, 1)


def kernel(**inputs):
    import numpy as np
    import concourse.bacc as bacc
    from concourse.bass_utils import run_bass_kernel_spmd

    src = np.pad(np.asarray(inputs["src"]), (0, EP - E))
    dst = np.pad(np.asarray(inputs["dst"]), (0, EP - E), constant_values=N)
    ea = np.pad(np.asarray(inputs["edge_attr_32"]), ((0, EP - E), (0, 0)))
    arrays = {name: np.ascontiguousarray(inputs[name]) for name in ["x", "L1_gnn_eps"] + ROWS + MATS + EDGE_MATS}
    arrays["src_chunks"] = np.ascontiguousarray(src.reshape(HALVES, CH, P).transpose(0, 2, 1))
    arrays["dst_chunks"] = np.ascontiguousarray(dst.reshape(HALVES, CH, P).transpose(0, 2, 1))
    arrays["dst_line"] = dst
    arrays["edge_attr_halves"] = np.ascontiguousarray(ea.reshape(HALVES, HALF, DE).transpose(0, 2, 1))

    nc = bacc.Bacc("TRN2", target_bir_lowering=False, num_devices=1)
    aps = {}
    for name, v in arrays.items():
        dt = U32 if name == "src_chunks" else mybir.dt.from_np(v.dtype)
        aps[name] = nc.dram_tensor(f"in_{name}", v.shape, dt, kind="ExternalInput").ap()
    out = nc.dram_tensor("out_x", (N, D), F32, kind="ExternalOutput").ap()
    gnn_program(nc, aps, out)
    r = run_bass_kernel_spmd(nc, [{f"in_{k}": v for k, v in arrays.items()}], core_ids=[0])
    return r.results[0]["out_x"]
```

```python
from contextlib import ExitStack

import concourse.bass as bass
from concourse import mybir

P = 128
N = 6250
E = 200000
D = 96
DE = 32
NT = (N + P - 1) // P
GT = 4
NG = (NT + GT - 1) // GT
TT = NG * GT
TAIL = N - (NT - 1) * P
QUAD = 4 * P
CH = 16
HALF = CH * P
BODIES = (E + 2 * HALF - 1) // (2 * HALF)
HALVES = 2 * BODIES
EP = HALVES * HALF
SLOTS = 8
EPS = 1e-5
NEG = -3.38e38
SUM, MAX = 0, 1
W = 8
WPT = P // W
WINDOWS = NT * WPT
READ = 3
KEYW = 512
BLOCK = 32
BLOCKS = HALF // BLOCK
PAIR = 2
POOL_LOADS = 4
ABLK = NT * P
SPLIT = (NT + 1) // 2
RING = 4
PARTS = 3
assert NT * W <= KEYW and NT % 2 == 1 and READ * P % BLOCK == 0 and NT % RING == 1 and NG % 2 == 1

ALU = mybir.AluOpType
ACT = mybir.ActivationFunctionType
AX = mybir.AxisListType
F32 = mybir.dt.float32
BF16 = mybir.dt.bfloat16
F16 = mybir.dt.float16
I32 = mybir.dt.int32
U32 = mybir.dt.uint32

ROWS = ["L0_gnn_ln_in_w", "L0_gnn_ln_in_b", "L0_gnn_b1", "L0_gnn_b2", "L0_gnn_ln_out_w", "L0_gnn_ln_out_b",
        "L1_gnn_b1", "L1_gnn_b2", "L1_gnn_gamma", "L1_gnn_beta", "L2_gnn_b0", "L2_gnn_g0", "L2_gnn_be0",
        "L2_gnn_b1", "L2_gnn_g1", "L2_gnn_be1", "L3_gnn_b1", "L3_gnn_b2"]
MATS = ["L0_gnn_W1", "L0_gnn_W2", "L1_gnn_W1", "L1_gnn_W2", "L2_gnn_W0", "L2_gnn_W1", "L3_gnn_W1_msg",
        "L3_gnn_W1_root", "L3_gnn_W2_msg", "L3_gnn_W2_root"]
EDGE_MATS = ["L3_gnn_W1_edge", "L3_gnn_W2_edge"]
KINDS = [SUM, SUM, SUM, SUM, SUM, MAX, MAX]


def gnn_program(nc, a, out):
    with ExitStack() as ctx:
        def sb(name, shape, dt=F32):
            return ctx.enter_context(nc.sbuf_tensor(name, shape, dt))

        def ps(name, shape, dt=F32):
            return ctx.enter_context(nc.psum_tensor(name, shape, dt))

        def sem(name):
            return ctx.enter_context(nc.semaphore(name))

        table_d = nc.dram_tensor("table_scratch", (NT * P, D), F32, kind="Internal").ap()
        scan_d = nc.dram_tensor("scan_scratch", (EP, D), F32, kind="Internal").ap()
        flag_d = [nc.dram_tensor(f"flag_scratch_{n}", (HALVES, HALF), BF16, kind="Internal").ap()
                  for n in ("sum", "max")]

        keys_d = nc.dram_tensor("edge_keys_scratch", (EP, 2), F32, kind="Internal").ap()
        adj_d = nc.dram_tensor("adjacency_scratch", (NT * P, ABLK), BF16, kind="Internal").ap()

        X = sb("X", [P, TT, D])
        H = sb("H", [P, TT, D])
        U = sb("U", [P, TT, D])
        V = sb("V", [P, TT, D])
        Z = sb("Z", [P, TT, D])
        rows = sb("rows", [P, len(ROWS), D])
        mats = sb("mats", [D, len(MATS), D])
        emats = sb("emats", [DE, 2, D])
        gin_eps = sb("gin_eps", [P, 1])
        iota_i = sb("iota_i", [P, P], I32)
        part_i = sb("part_i", [P, 1], I32)
        iota_f = sb("iota_f", [P, P])
        iota_b = sb("iota_b", [P, P], BF16)
        part_f = sb("part_f", [P, 1])
        ident = sb("ident", [P, P])
        upper = sb("upper", [P, P])
        ones = sb("ones", [P, P])
        real_row = sb("real_row", [P, 1])
        zero_b = sb("zero_b", [P, P], BF16)
        count = sb("count", [P, TT])
        upto = sb("upto", [P, TT])
        colsum = sb("colsum", [P, TT])
        has_edge = sb("has_edge", [P, TT])
        dinv = sb("dinv", [P, TT])
        last_row = sb("last_row", [P, TT], U32)
        last_a = sb("last_a", [P, TT], I32)
        last_b = sb("last_b", [P, TT], I32)
        mean = sb("mean", [P, TT])
        rstd = sb("rstd", [P, TT])
        bn_a = sb("bn_a", [P, D])
        bn_b = sb("bn_b", [P, D])
        bn_c = sb("bn_c", [P, D])
        ones_b = sb("ones_b", [P, 1], BF16)
        first_edge = sb("first_edge", [1, WINDOWS], I32)
        read_blocks = sb("read_blocks", [1, WINDOWS])
        windows_f = sb("windows_f", [1, 1])
        windows_i = sb("windows_i", [1, 1], I32)
        real_count = sb("real_count", [P, TT])
        most = sb("most", [P, 1])
        regular_f = sb("regular_f", [1, 1])
        regular_i = sb("regular_i", [1, 1], I32)
        stage = sb("stage", [P, 2, GT, D])
        yT = sb("yT", [D, 2, GT * P])

        region = sb("region", [P, (RING * ABLK + NT * PARTS * D) // 2])
        used = [0]

        def carve(parts, shape, dt=F32):
            size = 1
            for n in shape:
                size *= n
            words = size // (2 if dt == BF16 else 1)
            piece = region[0:parts, used[0]:used[0] + words]
            used[0] += words
            if dt != F32:
                piece = piece.bitcast(dt)
            names = "abcd"[:len(shape)]
            return piece.rearrange(f"p ({' '.join(names)}) -> p {' '.join(names)}",
                                   **{n: v for n, v in zip(names[1:], shape[1:])})

        adj = carve(P, [RING, NT, P], BF16)
        parts = carve(P, [NT, PARTS, D], BF16)
        used[0] = 0
        idx = carve(P, [2, CH], U32)
        keep = carve(D, [2, HALF], BF16)
        ea = carve(DE, [2, HALF])
        ring = carve(P, [SLOTS * 4, D])
        scan = carve(D, [2, QUAD])
        stored = carve(P, [2, CH, D])
        used[0] = 0
        hot_lo = carve(P, [2, CH, P], BF16)
        hot_hi = carve(P, [2, CH, 64], BF16)
        same = carve(HALVES, [HALF], BF16)
        newseg = carve(HALVES, [HALF], BF16)
        src_i = carve(HALVES, [HALF], I32)
        key_i = carve(HALVES, [HALF], I32)
        key_t = carve(HALVES, [HALF], I32)
        used[0] += 1024
        set_up_end = used[0]
        window_h = carve(P, [WINDOWS], BF16).bitcast(F16)
        window_key = carve(P, [WINDOWS])
        window_i = carve(P, [WINDOWS], I32)
        window_key_i = carve(P, [WINDOWS], I32)
        place_rep = carve(P, [P, PAIR * READ], BF16)
        place_rep_i = carve(P, [P, PAIR * READ], I32)
        later = carve(HALVES, [2, 2, WINDOWS], BF16)
        end_i = carve(HALVES, [2, BLOCKS], I32)
        end_f = carve(HALVES, [2, BLOCKS])
        place_h = window_h[:, 0:NT * W]
        used[0] = 0
        built = carve(P, [2, NT, P], BF16)
        hot_src = carve(P, [4, P, PAIR * READ], BF16)
        hot_key = carve(P, [4, READ, NT * W], BF16)
        keys = carve(P, [2, WPT * READ, 2])
        own_key = carve(P, [2, WPT * READ])
        place_b = carve(P, [2, WPT * READ], BF16)
        assert used[0] <= set_up_end
        dst_i = H[:, :, :].rearrange("p t d -> p (t d)").bitcast(I32)[:, 0:HALVES * CH]
        lo_i = H[:, :, :].rearrange("p t d -> p (t d)").bitcast(I32)[:, HALVES * CH:2 * HALVES * CH]
        lo_f = U[:, :, :].rearrange("p t d -> p (t d)")[:, 0:HALVES * CH]
        hi_f = U[:, :, :].rearrange("p t d -> p (t d)")[:, HALVES * CH:2 * HALVES * CH]
        cur_i = V[:, :, :].rearrange("p t d -> p (t d)").bitcast(I32)[0:HALVES, 0:HALF]
        prev_i = V[:, :, :].rearrange("p t d -> p (t d)").bitcast(I32)[0:HALVES, HALF:2 * HALF]
        edge_keys = Z[:, :, :].rearrange("p t d -> p (t d)")[0:HALVES, 0:2 * HALF].rearrange("p (e k) -> p e k", k=2)
        psF = [ps(f"psF{i}", [P, QUAD]) for i in range(2)]
        psB = [ps(f"psB{i}", [P, QUAD]) for i in range(2)]
        psT = ps("psT", [P, QUAD])
        psM = ps("psM", [P, QUAD])
        psX = ps("psX", [P, QUAD])
        banks = [psF[0], psF[1], psB[0], psB[1]]

        s_param = sem("params_loaded")
        s_x = sem("x_loaded")
        s_dst = sem("dst_loaded")
        s_prev = sem("prev_loaded")
        s_iota = sem("iota_made")
        s_const = sem("consts_made")
        s_flag = sem("flags_made")
        s_flagw = sem("flags_written")
        s_lohi = sem("lo_hi_made")
        s_hot = sem("one_hots_made")
        s_hotu = sem("one_hots_used")
        s_hist = sem("histogram_done")
        s_cnt = sem("count_copied")
        s_pre = sem("prefix_done")
        s_v = sem("vector_chain")
        s_to_act = sem("vector_to_scalar")
        s_from_act = sem("scalar_to_vector")
        s_to_pe = sem("vector_to_tensor")
        s_from_pe = sem("tensor_to_vector")
        s_src = sem("src_loaded")
        s_keys = sem("edge_keys_made")
        s_keysw = sem("edge_keys_written")
        s_later = sem("block_ends_compared")
        s_lateru = sem("block_ends_counted")
        s_windows = sem("window_reads_decided")
        s_most = sem("most_edges_made")
        s_mostt = sem("most_edges_turned")
        s_mode = sem("mode_decided")
        s_kl = [sem(f"keys_landed_{b}") for b in range(2)]
        s_pkl = [sem(f"keys_landed_by_pool_{b}") for b in range(2)]
        s_prep = sem("window_keys_made_relative")
        s_deg = sem("degrees_done")
        s_hotw = sem("window_one_hots_made")
        s_win = sem("window_counts_done")
        s_wev = sem("window_counts_copied")
        s_ast = [sem(f"adjacency_stored_{h}") for h in range(2)]
        s_at = [sem(f"adjacency_landed_{r}") for r in range(RING)]
        s_left = sem("table_or_remainder_ready")
        s_cut = sem("part_rounded")
        s_dag = sem("product_done")
        s_dev = sem("product_summed")
        s_turn = sem("turns")

        class EdgeSems:

            def __init__(self, kind):
                self.tbl = sem(f"{kind}_table_ready")
                self.tblw = sem(f"{kind}_table_written")
                self.idx = [sem(f"{kind}_idx_landed_{h}") for h in range(2)]
                self.keep = [sem(f"{kind}_keep_landed_{h}") for h in range(2)]
                self.ea = [sem(f"{kind}_edge_attr_landed_{h}") for h in range(2)]
                self.g = [sem(f"{kind}_gathered_{s}") for s in range(SLOTS)]
                self.fwd = sem(f"{kind}_feature_major_done")
                self.scan = sem(f"{kind}_scan_done")
                self.back = sem(f"{kind}_edge_major_done")
                self.evac = sem(f"{kind}_edge_major_copied")
                self.st = [sem(f"{kind}_scan_stored_{h}") for h in range(2)]
                self.agg = sem(f"{kind}_aggregates_landed")

        edge_sems = [EdgeSems("sum"), EdgeSems("max")]

        def conv_sems(k):
            return edge_sems[KINDS[k]], k - (5 if KINDS[k] == MAX else 0)

        s_lin = sem("linear_input_ready")
        s_stage = sem("linear_staged")
        s_lt = sem("linear_transposed")
        s_yt = sem("linear_transpose_copied")
        s_lm = sem("linear_product_done")
        s_lo = sem("linear_product_copied")
        s_outr = sem("output_ready")
        s_out = sem("output_stored")

        def node(t):
            return t[:, 0:NT, :]

        def per_node(t):
            return t[:, 0:NT].unsqueeze(2).to_broadcast([P, NT, D])

        def per_feature(t):
            return t.unsqueeze(1).to_broadcast([P, NT, D])

        def row(name):
            return rows[:, ROWS.index(name), :]

        def mat(name):
            return mats[:, MATS.index(name), :]

        LIN = [(U, "L0_gnn_W1", V), (U, "L0_gnn_W2", V), (U, "L1_gnn_W1", V), (U, "L1_gnn_W2", V),
               (H, "L2_gnn_W0", V), (H, "L2_gnn_W1", V), (H, "L3_gnn_W1_msg", V), (H, "L3_gnn_W1_root", U),
               (H, "L3_gnn_W2_msg", V), (H, "L3_gnn_W2_root", U)]
        NODE_HALVES = [(0, SPLIT), (SPLIT, NT)]
        STEPS = [("lin", 0), ("conv", 0), ("lin", 1), ("conv", 1), ("conv", 2), ("lin", 2), ("lin", 3),
                 ("lin", 4), ("conv", 3), ("lin", 5), ("conv", 4),
                 ("lin", 6), ("lin", 7), ("conv", 5), ("lin", 8), ("lin", 9), ("conv", 6)]

        def adj_tile(d):
            return adj_d.rearrange("(d p) m -> d p m", p=P)[bass.ds(d, 1), :, :].rearrange("a p m -> p (a m)")

        def tile_pairs(eng, step):
            step(0, 0, 0)
            with eng.Fori(0, NT // 2) as i:
                step(i * 2 + 1, 1, i)
                step(i * 2 + 2, 0, i + 1)

        def load_window(eng, d, buf, j, landed):
            first = eng.value_load(first_edge[0:1, bass.ds(d * WPT + j, 1)], min_val=0, max_val=EP - READ * P)
            eng.dma_start(keys[:, buf, j * READ:(j + 1) * READ, :].rearrange("p c k -> p (c k)"),
                          keys_d[bass.ds(first, READ * P), :].rearrange("(p c) k -> p (c k)", c=READ)
                          ).then_inc(landed[buf], 16)

        block = ctx.enter_context(nc.Block())

        @block.sync
        def _(sp):
            sp.dma_start(dst_i, a["dst_chunks"].rearrange("h p c -> p h c")).then_inc(s_dst, 16)
            sp.dma_start(cur_i, a["dst_line"].rearrange("(h e) -> h e", e=HALF)).then_inc(s_prev, 16)
            sp.dma_start(src_i, a["src_line"].rearrange("(h e) -> h e", e=HALF)).then_inc(s_src, 16)
            sp.wait_ge(s_v, 2)
            sp.dma_start(prev_i[0:1, 1:HALF], a["dst_line"][0:HALF - 1].unsqueeze(0)).then_inc(s_prev, 16)
            sp.dma_start(prev_i[1:HALVES, :], a["dst_line"][HALF - 1:EP - 1].rearrange("(h e) -> h e", e=HALF)
                         ).then_inc(s_prev, 16)
            sp.dma_start(X[:, 0:NT - 1, :], a["x"][0:(NT - 1) * P, :].rearrange("(t p) d -> p t d", p=P)
                         ).then_inc(s_x, 16)
            sp.dma_start(X[0:TAIL, NT - 1, :], a["x"][(NT - 1) * P:N, :]).then_inc(s_x, 16)
            for i, name in enumerate(ROWS):
                sp.dma_start(rows[:, i, :], a[name].partition_broadcast(P)).then_inc(s_param, 16)
            for i, name in enumerate(MATS):
                sp.dma_start(mats[:, i, :], a[name]).then_inc(s_param, 16)
            for i, name in enumerate(EDGE_MATS):
                sp.dma_start(emats[:, i, :], a[name]).then_inc(s_param, 16)
            sp.dma_start(gin_eps[:, :], a["L1_gnn_eps"].partition_broadcast(P)).then_inc(s_param, 16)
            sp.wait_ge(s_flag, 1)
            sp.dma_start(flag_d[SUM], same).then_inc(s_flagw, 16)
            sp.dma_start(flag_d[MAX], newseg).then_inc(s_flagw, 16)
            sp.wait_ge(s_keys, 1)
            sp.dma_start(keys_d.rearrange("(h e) k -> h (e k)", e=HALF), edge_keys.rearrange("p e k -> p (e k)")
                         ).then_inc(s_keysw, 16)
            sp.wait_ge(s_flagw, 32)
            sp.wait_ge(s_keysw, 16)
            sp.wait_ge(s_windows, 1)
            windows_fit = sp.value_load(windows_i[0:1, 0:1], min_val=0, max_val=1)

            def build_loads():
                def load_windows(d, buf, turn):
                    sp.wait_ge(s_prep, d + 1)
                    sp.sem_inc(s_turn, 1)
                    for j in range(POOL_LOADS, WPT):
                        load_window(sp, d, buf, j, s_kl)

                tile_pairs(sp, load_windows)
                sp.wait_ge(s_ast[0], 16 * (NT // 2 + 2))
                sp.wait_ge(s_ast[1], 16 * (NT // 2 + 1))

            with sp.If(windows_fit == 1):
                build_loads()
            sp.wait_ge(s_mode, 1)
            mode = sp.value_load(regular_i[0:1, 0:1], min_val=0, max_val=1)

            def product_loads(k):
                sp.wait_ge(s_dag, NT * k + RING)
                with sp.Fori(0, NT // RING) as i:
                    for r in range(RING):
                        d = sp.snap(i * RING + r)
                        sp.wait_ge(s_dag, i * RING + (NT * k + r + 1))
                        sp.sem_inc(s_turn, 1)
                        sp.dma_start(adj[:, r, :, :].rearrange("p t c -> p (t c)"), adj_tile(d)
                                     ).then_inc(s_at[r], 16)
                sp.wait_ge(s_dag, NT * k + NT)
                sp.dma_start(adj[:, 0, :, :].rearrange("p t c -> p (t c)"), adj_tile(NT - 1)
                             ).then_inc(s_at[0], 16)

            def conv_loads(k):
                kind = KINDS[k]
                s_, n = conv_sems(k)
                base = 8 * BODIES * n
                sp.wait_ge(s_.tbl, n + 1)
                sp.dma_start(table_d.rearrange("(t p) d -> p t d", p=P), node(H if k == 2 else V)
                             ).then_inc(s_.tblw, 16)
                with sp.Fori(0, BODIES) as it:
                    for h in range(2):
                        half = sp.snap(it * 2 + h)
                        sp.wait_ge(s_.fwd, it * 8 + (base + 4 * h + 4))
                        sp.wait_ge(s_.scan, it * 8 + (base + 4 * h + 4))
                        sp.sem_inc(s_turn, 1)
                        sp.dma_start(idx[:, h, :], a["src_chunks"][bass.ds(half, 1), :, :].rearrange("a p c -> p (a c)")
                                     ).then_inc(s_.idx[h], 16)
                        sp.dma_start(keep[:, h, :], flag_d[kind][bass.ds(half, 1), :].rearrange("a e -> (a e)")
                                     .partition_broadcast(D)).then_inc(s_.keep[h], 16)
                        if kind == MAX:
                            sp.dma_start(ea[:, h, :], a["edge_attr_halves"][bass.ds(half, 1), :, :].rearrange(
                                "a f e -> f (a e)")).then_inc(s_.ea[h], 16)

            with sp.If(mode == 1):
                for k in range(5):
                    product_loads(k)
            with sp.Else():
                for k in range(5):
                    conv_loads(k)
            for k in (5, 6):
                conv_loads(k)
            sp.wait_ge(s_outr, 1)
            sp.dma_start(out[0:(NT - 1) * P, :].rearrange("(t p) d -> p t d", p=P), X[:, 0:NT - 1, :]
                         ).then_inc(s_out, 16)
            sp.dma_start(out[(NT - 1) * P:N, :], X[0:TAIL, NT - 1, :]).then_inc(s_out, 16)
            sp.wait_ge(s_out, 32)

        @block.gpsimd
        def _(pool):
            nc.gpsimd.iota(iota_i[:, :], pattern=[[1, P]], base=0, channel_multiplier=0).then_inc(s_iota, 1)
            nc.gpsimd.iota(part_i[:, :], pattern=[[0, 1]], base=0, channel_multiplier=1).then_inc(s_iota, 1)
            nc.gpsimd.iota(window_i, pattern=[[1, WINDOWS]], base=0, channel_multiplier=0).then_inc(s_iota, 1)
            nc.gpsimd.iota(window_key_i, pattern=[[KEYW, WINDOWS]], base=0, channel_multiplier=0).then_inc(s_iota, 1)
            nc.gpsimd.iota(place_rep_i, pattern=[[1, P], [0, PAIR * READ]], base=0, channel_multiplier=0
                           ).then_inc(s_iota, 1)
            pool.sem_inc(s_prep, 2)
            pool.wait_ge(s_windows, 1)
            windows_fit = pool.value_load(windows_i[0:1, 0:1], min_val=0, max_val=1)

            def load_windows(d, buf):
                pool.wait_ge(s_prep, d + 1)
                pool.sem_inc(s_turn, 1)
                for j in range(POOL_LOADS):
                    load_window(pool, d, buf, j, s_pkl)

            def relative_keys(d, buf, turn):
                pool.wait_ge(s_kl[buf], turn * (16 * (WPT - POOL_LOADS)) + 16 * (WPT - POOL_LOADS))
                pool.wait_ge(s_pkl[buf], turn * (16 * POOL_LOADS) + 16 * POOL_LOADS)
                pool.wait_ge(s_hotw, d * WPT + WPT)
                pool.sem_inc(s_turn, 1)
                own_window = window_key[:, bass.ds(d * WPT, WPT)].unsqueeze(2).to_broadcast([P, WPT, READ])
                nc.gpsimd.tensor_tensor(own_key[:, buf, :].rearrange("p (j c) -> p j c", c=READ),
                                        keys[:, buf, :, 0].rearrange("p (j c) -> p j c", c=READ),
                                        own_window, ALU.subtract)
                nc.gpsimd.tensor_copy(place_b[:, buf, :], keys[:, buf, :, 1]).then_inc(s_prep, 1)

            with pool.If(windows_fit == 1):
                load_windows(0, 0)
                with pool.Fori(0, NT // 2) as i:
                    load_windows(i * 2 + 1, 1)
                    relative_keys(i * 2, 0, i)
                    load_windows(i * 2 + 2, 0)
                    relative_keys(i * 2 + 1, 1, i)
                relative_keys(NT - 1, 0, NT // 2)
            pool.wait_ge(s_mode, 1)
            mode = pool.value_load(regular_i[0:1, 0:1], min_val=0, max_val=1)

            def gathers(k):
                s_, n = conv_sems(k)
                pool.wait_ge(s_.tblw, 16 * (n + 1))
                with pool.Fori(0, BODIES) as it:
                    for h in range(2):
                        pool.wait_ge(s_.idx[h], it * 16 + (16 * BODIES * n + 16))
                        pool.wait_ge(s_.fwd, it * 8 + (8 * BODIES * n + 4 * h + 4))
                        pool.sem_inc(s_turn, 1)
                        for c in range(CH):
                            nc.gpsimd.indirect_dma_start(
                                ring[:, h * CH + c, :], None, table_d,
                                bass.IndirectOffsetOnAxis(ap=idx[:, h, c:c + 1], axis=0)
                            ).then_inc(s_.g[4 * h + c // 4], 16)
                pool.wait_ge(s_.st[0], 16 * (BODIES * (n + 1) + 1))
                pool.wait_ge(s_.st[1], 16 * (BODIES * (n + 1) + 1))
                for t in range(NT):
                    nc.gpsimd.indirect_dma_start(
                        Z[:, t, :], None, scan_d, bass.IndirectOffsetOnAxis(ap=last_row[:, t:t + 1], axis=0)
                    ).then_inc(s_.agg, 16)

            with pool.If(mode == 0):
                for k in range(5):
                    gathers(k)
            for k in (5, 6):
                gathers(k)

        @block.tensor
        def _(pe):
            for s_ in edge_sems:
                pe.sem_inc(s_.fwd, 8)
                pe.sem_inc(s_.back, 2)
            pe.sem_inc(s_win, 4)
            pe.sem_inc(s_deg, 2)
            pe.sem_inc(s_lateru, 2)
            pe.sem_inc(s_dag, RING)
            pe.sem_inc(s_hotu, 2)
            pe.sem_inc(s_lt, 2)
            pe.sem_inc(s_lm, 2)
            pe.wait_ge(s_const, 1)
            half_w = WINDOWS // 2

            def count_blocks(c, b, start, stop):
                pe.wait_ge(s_later, c + 1)
                for end, of_end in enumerate((psF, psB)):
                    for bank in range(2):
                        last = nc.tensor.matmul(of_end[bank][0:1, 0:half_w], ones_b[0:HALVES, :],
                                                later[:, b, end, bank * half_w:(bank + 1) * half_w],
                                                start=start, stop=stop)
                last.then_inc(s_lateru, 1)

            count_blocks(0, 0, True, False)
            with pe.Fori(0, BLOCKS // 2 - 1) as i:
                count_blocks(i * 2 + 1, 1, False, False)
                count_blocks(i * 2 + 2, 0, False, False)
            count_blocks(BLOCKS - 1, 1, False, True)
            pe.wait_ge(s_windows, 1)
            windows_fit = pe.value_load(windows_i[0:1, 0:1], min_val=0, max_val=1)

            def build():
                def degrees(d, buf):
                    pe.wait_ge(s_wev, d * WPT + (WPT + 4))
                    for t in range(NT):
                        last = nc.tensor.matmul(psX[:, bass.ds(d, 1)], built[:, buf, t, :], ones_b[:, :],
                                                start=(t == 0), stop=(t == NT - 1))
                    last.then_inc(s_deg, 1)

                def count_windows(d, buf, before=None):
                    for j in range(WPT):
                        pe.wait_ge(s_hotw, d * WPT + (j + 2 * WPT + 1))
                        pe.wait_ge(s_wev, d * WPT + (j + 1))
                        for c in range(READ):
                            last = nc.tensor.matmul(banks[j % 4][:, 0:NT * W],
                                                    hot_src[:, j // PAIR % 4, :, j % PAIR * READ + c],
                                                    hot_key[:, j % 4, c, :],
                                                    start=(c == 0), stop=(c == READ - 1))
                        last.then_inc(s_win, 1)
                        if j == WPT // 2 and before is not None:
                            degrees(before, 1 - buf)

                count_windows(0, 0)
                with pe.Fori(0, NT // 2) as i:
                    count_windows(i * 2 + 1, 1, i * 2)
                    count_windows(i * 2 + 2, 0, i * 2 + 1)
                degrees(NT - 1, 0)
                pe.wait_ge(s_most, 1)
                nc.tensor.transpose(psT[0:1, 0:P], most[:, :], ident[:, :]).then_inc(s_mostt, 1)

            def histogram():
                hist = psX[:, 0:64]
                nc.tensor.matmul(hist, zero_b[:, :], zero_b[:, 0:64], start=True, stop=False)
                with pe.Fori(0, BODIES) as it:
                    for h in range(2):
                        pe.wait_ge(s_hot, it * 2 + (h + 1))
                        for c in range(CH):
                            last = nc.tensor.matmul(hist, hot_lo[:, h, c, :], hot_hi[:, h, c, :], start=False,
                                                    stop=False)
                        last.then_inc(s_hotu, 1)
                nc.tensor.matmul(hist, zero_b[:, :], zero_b[:, 0:64], start=False, stop=True).then_inc(s_hist, 1)

            with pe.If(windows_fit == 1):
                build()
            pe.wait_ge(s_mode, 1)
            mode = pe.value_load(regular_i[0:1, 0:1], min_val=0, max_val=1)
            with pe.If(mode == 0):
                histogram()
            pe.wait_ge(s_cnt, 1)
            nc.tensor.matmul(psT[:, 0:TT], upper[:, :], count[:, :], start=True, stop=True)
            nc.tensor.matmul(psM[:, 0:TT], ones[:, :], count[:, :], start=True, stop=True).then_inc(s_pre, 1)

            def product(k):
                pe.wait_ge(s_cut, 6 * (k + 1))

                def tile(i, r, landed):
                    pe.wait_ge(s_at[r], landed)
                    pe.wait_ge(s_dev, i * RING + (NT * k + r + 1))
                    for t in range(NT):
                        last = nc.tensor.matmul(psF[r % 2][:, 0:PARTS * D], adj[:, r, t, :],
                                                parts[:, t, :, :].rearrange("p s d -> p (s d)"),
                                                start=(t == 0), stop=(t == NT - 1))
                    last.then_inc(s_dag, 1)

                full = NT // RING
                with pe.Fori(0, full) as i:
                    for r in range(RING):
                        tile(i, r, i * 16 + 16 * ((full + (r == 0)) * k + 1))
                tile(full, 0, 16 * (full + 1) * (k + 1))

            def linear(j):
                src, w, dst = LIN[j]
                base = NG * j

                def turn(g, b):
                    pe.wait_ge(s_stage, g + (base + 1))
                    pe.wait_ge(s_yt, g + (base + 1))
                    for t in range(GT):
                        last = nc.tensor.transpose(psF[b][0:D, t * P:(t + 1) * P], stage[:, b, t, :], ident[:, :])
                    last.then_inc(s_lt, 1)

                def multiply(g, b):
                    pe.wait_ge(s_yt, g + (base + 3))
                    pe.wait_ge(s_lo, g + (base + 1))
                    for t in range(GT):
                        last = nc.tensor.matmul(psB[b][:, t * D:(t + 1) * D], yT[:, b, t * P:(t + 1) * P], mat(w),
                                                start=True, stop=True)
                    last.then_inc(s_lm, 1)

                turn(0, 0)
                with pe.Fori(0, NG // 2) as i:
                    turn(i * 2 + 1, 1)
                    multiply(i * 2, 0)
                    turn(i * 2 + 2, 0)
                    multiply(i * 2 + 1, 1)
                multiply(NG - 1, 0)
                pe.wait_ge(s_lo, base + NG + 2)

            def conv(k):
                s_, n = conv_sems(k)
                base = 8 * BODIES * n

                def feature_major(it, s):
                    h, q, b = s // 4, s % 4, s % 2
                    pe.wait_ge(s_.scan, it * 8 + (base + s + 7))
                    pe.wait_ge(s_.g[s], it * 64 + (64 * BODIES * n + 64))
                    if KINDS[k] == MAX:
                        pe.wait_ge(s_.ea[h], it * 16 + (16 * BODIES * n + 16))
                        nc.tensor.matmul(psF[b][0:D, :], emats[:, n, :], ea[:, h, q * QUAD:(q + 1) * QUAD],
                                         start=True, stop=False)
                    for c in range(4):
                        rows_in = ring[:, 4 * s + c, :]
                        if KINDS[k] == MAX:
                            last = nc.tensor.matmul(psF[b][0:D, c * P:(c + 1) * P], rows_in, ident[:, :],
                                                    start=False, stop=(c == 3))
                        else:
                            last = nc.tensor.transpose(psF[b][0:D, c * P:(c + 1) * P], rows_in, ident[:, :])
                    last.then_inc(s_.fwd, 1)

                def edge_major(it, s):
                    b = s % 2
                    pe.wait_ge(s_.scan, it * 8 + (base + s + 9))
                    pe.wait_ge(s_.evac, it * 8 + (base + s + 1))
                    for c in range(4):
                        last = nc.tensor.transpose(psB[b][:, c * D:(c + 1) * D], scan[:, b, c * P:(c + 1) * P],
                                                   ident[0:D, 0:D])
                    last.then_inc(s_.back, 1)

                with pe.Fori(0, BODIES) as it:
                    feature_major(it, 0)
                    for s in range(SLOTS):
                        if s + 1 < SLOTS:
                            feature_major(it, s + 1)
                        edge_major(it, s)

            pe.wait_ge(s_param, 16 * (len(ROWS) + len(MATS) + len(EDGE_MATS) + 1))
            for what, n in STEPS:
                if what == "lin":
                    linear(n)
                elif KINDS[n] == MAX:
                    conv(n)
                else:
                    with pe.If(mode == 1):
                        product(n)
                    with pe.Else():
                        conv(n)
                if (what, n) == ("lin", 3):
                    for i in range(2):
                        pe.wait_ge(s_to_pe, i + 1)
                        nc.tensor.matmul(psX[:, i * D:(i + 1) * D], ones[:, :], bn_a[:, :], start=True, stop=True
                                         ).then_inc(s_from_pe, 1)

        @block.scalar
        def _(act):
            for s_ in edge_sems:
                act.sem_inc(s_.evac, 2)
                act.sem_inc(s_.st[0], 16)
                act.sem_inc(s_.st[1], 16)
            act.sem_inc(s_wev, 4)
            act.sem_inc(s_yt, 2)
            act.sem_inc(s_ast[0], 16)
            act.sem_inc(s_ast[1], 16)
            handed = [0]

            def from_vector(call):
                handed[0] += 1
                act.wait_ge(s_to_act, handed[0])
                call().then_inc(s_from_act, 1)

            def square_and_root(t):
                from_vector(lambda: nc.scalar.activation(node(Z), node(t), ACT.Square))
                from_vector(lambda: nc.scalar.activation(rstd[:, 0:NT], rstd[:, 0:NT], ACT.Sqrt))

            def linear(j):
                src, w, dst = LIN[j]
                base = NG * j
                act.wait_ge(s_lin, j + 1)

                def stage_group(g, b):
                    act.wait_ge(s_lt, g + (base + 1))
                    nc.scalar.copy(stage[:, b, :, :], src[:, bass.ds(g * GT, GT), :]).then_inc(s_stage, 1)

                def copy_turned(g, b):
                    act.wait_ge(s_lt, g + (base + 3))
                    act.wait_ge(s_lm, g + (base + 1))
                    nc.scalar.copy(yT[:, b, :], psF[b][0:D, :]).then_inc(s_yt, 1)

                stage_group(0, 0)
                with act.Fori(0, NG // 2) as i:
                    stage_group(i * 2 + 1, 1)
                    copy_turned(i * 2, 0)
                    stage_group(i * 2 + 2, 0)
                    copy_turned(i * 2 + 1, 1)
                copy_turned(NG - 1, 0)

            def cut(k):
                table = H if k == 2 else V
                for part in range(PARTS):
                    for half, (t0, t1) in enumerate(NODE_HALVES):
                        if (part, half) == (0, 0):
                            act.wait_ge(s_left, 5 * k + 1)
                        elif part > 0:
                            act.wait_ge(s_left, 5 * k + 2 * part + half)
                        of = table if part == 0 else Z
                        nc.scalar.copy(parts[:, t0:t1, part, :], of[:, t0:t1, :]).then_inc(s_cut, 1)

            def build():
                def collect(d, buf, turn):
                    act.wait_ge(s_ast[buf], turn * 16 + 16)
                    act.wait_ge(s_deg, d + 1)
                    for j in range(WPT):
                        act.wait_ge(s_win, d * WPT + (j + 5))
                        nc.scalar.copy(built[:, buf, :, j * W:(j + 1) * W],
                                       banks[j % 4][:, 0:NT * W].rearrange("p (t w) -> p t w", w=W)).then_inc(s_wev, 1)
                    act.wait_ge(s_wev, d * WPT + (WPT + 4))
                    act.dma_start(adj_tile(d), built[:, buf, :, :].rearrange("p t c -> p (t c)")
                                  ).then_inc(s_ast[buf], 16)

                tile_pairs(act, collect)

            def conv(k):
                s_, n = conv_sems(k)
                base = 8 * BODIES * n
                with act.Fori(0, BODIES) as it:
                    for s in range(SLOTS):
                        h, q, b = s // 4, s % 4, s % 2
                        if q == 0:
                            act.wait_ge(s_.st[h], it * 16 + (16 * BODIES * n + 16))
                        act.wait_ge(s_.back, it * 8 + (base + s + 3))
                        nc.scalar.copy(stored[:, h, q * 4:(q + 1) * 4, :],
                                       psB[b][:, 0:4 * D].rearrange("p (c d) -> p c d", d=D)).then_inc(s_.evac, 1)
                        if q == 3:
                            act.wait_ge(s_.evac, it * 8 + (base + s + 3))
                            act.dma_start(
                                scan_d.rearrange("(i p c) d -> i p (c d)", p=P, c=CH)[bass.ds(it * 2 + h, 1), :, :]
                                .rearrange("a p m -> p (a m)"),
                                stored[:, h, :, :].rearrange("p c d -> p (c d)")).then_inc(s_.st[h], 16)

            act.wait_ge(s_windows, 1)
            windows_fit = act.value_load(windows_i[0:1, 0:1], min_val=0, max_val=1)
            with act.If(windows_fit == 1):
                build()
            act.wait_ge(s_mode, 1)
            mode = act.value_load(regular_i[0:1, 0:1], min_val=0, max_val=1)
            from_vector(lambda: nc.scalar.activation(dinv[:, 0:NT], dinv[:, 0:NT], ACT.Sqrt))

            def sums(k):
                with act.If(mode == 1):
                    cut(k)
                with act.Else():
                    conv(k)

            square_and_root(H)
            square_and_root(U)
            linear(0)
            sums(0)
            linear(1)
            sums(1)
            square_and_root(H)
            square_and_root(H)
            sums(2)
            linear(2)
            linear(3)
            from_vector(lambda: nc.scalar.activation(node(Z), node(V), ACT.Square))
            from_vector(lambda: nc.scalar.activation(bn_b[:, :], bn_b[:, :], ACT.Sqrt))
            square_and_root(H)
            linear(4)
            sums(3)
            from_vector(lambda: nc.scalar.activation(node(U), node(U), ACT.Tanh))
            square_and_root(H)
            linear(5)
            sums(4)
            from_vector(lambda: nc.scalar.activation(node(U), node(U), ACT.Tanh))
            square_and_root(H)
            square_and_root(H)
            for i in range(2):
                linear(6 + 2 * i)
                linear(7 + 2 * i)
                conv(5 + i)

        @block.vector
        def _(dve):
            chained, handed, to_pe = [0], [0], [0]
            V_ = nc.vector

            def link(ins):
                chained[0] += 1
                ins.then_inc(s_v, 1)
                dve.wait_ge(s_v, chained[0])

            def scalar_turn():
                handed[0] += 1
                dve.sem_inc(s_to_act, 1)
                dve.wait_ge(s_from_act, handed[0])

            link(V_.memset(prev_i[0:1, 0:1], -1))
            link(V_.memset(X[:, NT - 1:TT, :], 0.0))
            for t in (H, U, V):
                V_.memset(t[:, NT:TT, :], 0.0)
            for s_ in edge_sems:
                dve.sem_inc(s_.scan, 8)
            dve.sem_inc(s_hotw, 2 * WPT)
            dve.sem_inc(s_dev, 2)
            dve.sem_inc(s_lo, 2)
            V_.memset(zero_b[:, :], 0.0)
            V_.memset(ones[:, :], 1.0)
            V_.memset(ones_b[:, :], 1.0)
            dve.wait_ge(s_iota, 5)
            V_.tensor_copy(window_h, window_i)
            V_.tensor_copy(place_rep, place_rep_i)
            V_.tensor_copy(window_key, window_key_i)
            V_.tensor_copy(iota_f[:, :], iota_i[:, :])
            V_.tensor_copy(iota_b[:, :], iota_i[:, :])
            link(V_.tensor_copy(part_f[:, :], part_i[:, :]))
            V_.tensor_scalar(ident[:, :], iota_f[:, :], part_f[:, 0:1], None, ALU.is_equal)
            V_.tensor_scalar(upper[:, :], iota_f[:, :], part_f[:, 0:1], None, ALU.is_ge)
            V_.tensor_scalar(real_row[:, :], part_f[:, :], float(TAIL), None, ALU.is_lt).then_inc(s_const, 1)
            dve.wait_ge(s_prev, 48)
            link(V_.tensor_tensor(same, cur_i, prev_i, ALU.is_equal))
            V_.tensor_scalar(newseg, same, -NEG, NEG, ALU.mult, ALU.add).then_inc(s_flag, 1)
            dve.wait_ge(s_src, 16)
            window_bits, key_bits, place_bits = W.bit_length() - 1, KEYW.bit_length() - 1, 7
            link(V_.tensor_scalar(key_i, cur_i, window_bits, key_bits, ALU.logical_shift_right,
                                  ALU.logical_shift_left))
            link(V_.tensor_scalar(key_t, cur_i, W - 1, None, ALU.bitwise_and))
            link(V_.tensor_tensor(key_i, key_i, key_t, ALU.bitwise_or))
            link(V_.tensor_scalar(key_t, src_i, place_bits, window_bits, ALU.logical_shift_right,
                                  ALU.logical_shift_left))
            link(V_.tensor_tensor(key_i, key_i, key_t, ALU.bitwise_or))
            link(V_.tensor_copy(edge_keys[:, :, 0], key_i))
            link(V_.tensor_scalar(key_t, src_i, P - 1, None, ALU.bitwise_and))
            V_.tensor_copy(edge_keys[:, :, 1], key_t).then_inc(s_keys, 1)
            ends = cur_i.rearrange("p (b e) -> p b e", e=BLOCK)
            V_.tensor_scalar(end_i[:, 0, :], ends[:, :, BLOCK - 1], window_bits, None, ALU.logical_shift_right)
            link(V_.tensor_scalar(end_i[:, 1, :], ends[:, :, 0], window_bits, None, ALU.logical_shift_right))
            link(V_.tensor_copy(end_f, end_i))

            def compare_blocks(c, b):
                dve.wait_ge(s_lateru, c + 1)
                V_.tensor_scalar(later[:, b, 0, :], window_h[0:HALVES, :], end_f[:, 0, bass.ds(c, 1)], None, ALU.is_gt)
                V_.tensor_scalar(later[:, b, 1, :], window_h[0:HALVES, :], end_f[:, 1, bass.ds(c, 1)], None, ALU.is_ge
                                 ).then_inc(s_later, 1)

            with dve.Fori(0, BLOCKS // 2) as i:
                for b in range(2):
                    compare_blocks(i * 2 + b, b)
            dve.wait_ge(s_lateru, BLOCKS + 2)
            half_w = WINDOWS // 2
            for bank in range(2):
                part = slice(bank * half_w, (bank + 1) * half_w)
                link(V_.tensor_copy(read_blocks[:, part], psF[bank][0:1, 0:half_w]))
                V_.tensor_scalar(first_edge[:, part], read_blocks[:, part], float(BLOCK), float(EP - READ * P),
                                 ALU.mult, ALU.min)
                link(V_.tensor_tensor(read_blocks[:, part], psB[bank][0:1, 0:half_w], read_blocks[:, part],
                                      ALU.subtract))
            link(V_.tensor_reduce(windows_f[:, :], read_blocks[:, 0:WINDOWS - 1], AX.X, ALU.max))
            link(V_.tensor_scalar(windows_f[:, :], windows_f[:, :], float(READ * P // BLOCK), None, ALU.is_le))
            link(V_.tensor_copy(windows_i[:, :], windows_f[:, :]))
            dve.wait_ge(s_flagw, 32)
            dve.wait_ge(s_keysw, 16)
            dve.sem_inc(s_windows, 1)
            windows_fit = dve.value_load(windows_i[0:1, 0:1], min_val=0, max_val=1)

            def build():
                def one_hots(d, buf, turn):
                    dve.wait_ge(s_prep, d + 3)
                    for j in range(WPT):
                        dve.wait_ge(s_win, d * WPT + (j + 1))
                        if j % PAIR == 0:
                            places = place_b[:, buf, j * READ:(j + PAIR) * READ].unsqueeze(1)
                            V_.tensor_tensor(hot_src[:, j // PAIR % 4, :, :], place_rep,
                                             places.to_broadcast([P, P, PAIR * READ]), ALU.is_equal)
                        for c in range(READ):
                            e = j * READ + c
                            last = V_.tensor_scalar(hot_key[:, j % 4, c, :], place_h, own_key[:, buf, e:e + 1], None,
                                                    ALU.is_equal)
                        last.then_inc(s_hotw, 1)

                tile_pairs(dve, one_hots)
                dve.wait_ge(s_deg, NT + 2)
                V_.memset(count[:, NT:TT], 0.0)
                link(V_.tensor_copy(count[:, 0:NT], psX[:, 0:NT]))
                link(V_.tensor_copy(real_count[:, 0:NT], count[:, 0:NT]))
                link(V_.tensor_scalar(real_count[:, NT - 1:NT], real_count[:, NT - 1:NT], real_row[:, 0:1], None,
                                      ALU.mult))
                V_.tensor_reduce(most[:, :], real_count[:, 0:NT], AX.X, ALU.max).then_inc(s_most, 1)
                dve.wait_ge(s_mostt, 1)
                link(V_.tensor_reduce(regular_f[:, :], psT[0:1, 0:P], AX.X, ALU.max))
                link(V_.tensor_scalar(regular_f[:, :], regular_f[:, :], 256.0, None, ALU.is_lt))
                link(V_.tensor_copy(regular_i[:, :], regular_f[:, :]))
                dve.wait_ge(s_ast[0], 16 * (NT // 2 + 2))
                dve.wait_ge(s_ast[1], 16 * (NT // 2 + 1))

            def histogram():
                link(V_.memset(hot_hi, 0.0))
                dve.wait_ge(s_dst, 16)
                link(V_.tensor_scalar(lo_i, dst_i, P - 1, None, ALU.bitwise_and))
                link(V_.tensor_copy(lo_f, lo_i))
                link(V_.tensor_scalar(lo_i, dst_i, 7, None, ALU.logical_shift_right))
                link(V_.tensor_copy(hi_f, lo_i))
                with dve.Fori(0, BODIES) as it:
                    for h in range(2):
                        dve.wait_ge(s_hotu, it * 2 + (h + 1))
                        for c in range(CH):
                            e = it * (2 * CH) + (h * CH + c)
                            V_.tensor_scalar(hot_lo[:, h, c, :], iota_b[:, :], lo_f[:, bass.ds(e, 1)], None,
                                             ALU.is_equal)
                            last = V_.tensor_scalar(hot_hi[:, h, c, 0:TT], iota_b[:, 0:TT], hi_f[:, bass.ds(e, 1)],
                                                    None, ALU.is_equal)
                        last.then_inc(s_hot, 1)
                dve.wait_ge(s_hist, 1)
                link(V_.tensor_copy(count[:, :], psX[:, 0:TT]))

            link(V_.memset(regular_i[:, :], 0))
            before = chained[0]
            with dve.If(windows_fit == 1):
                build()
            after_build = chained[0]
            chained[0] = before
            with dve.Else():
                dve.sem_inc(s_v, after_build - before)
            chained[0] = after_build
            dve.sem_inc(s_mode, 1)
            mode = dve.value_load(regular_i[0:1, 0:1], min_val=0, max_val=1)
            before = chained[0]
            with dve.If(mode == 0):
                histogram()
            after_histogram = chained[0]
            with dve.Else():
                dve.sem_inc(s_v, after_histogram - before)
            dve.sem_inc(s_cnt, 1)
            V_.tensor_scalar(has_edge[:, :], count[:, :], 0.0, None, ALU.is_gt)
            link(V_.tensor_scalar(dinv[:, :], count[:, :], 1.0, None, ALU.add))
            scalar_turn()
            V_.reciprocal(dinv[:, 0:NT], dinv[:, 0:NT])
            dve.wait_ge(s_pre, 1)
            link(V_.tensor_copy(colsum[:, :], psM[:, 0:TT]))
            link(V_.tensor_tensor_scan(upto[:, :], ones[:, 0:TT], colsum[:, :], 0.0, ALU.mult, ALU.add))
            link(V_.tensor_tensor(upto[:, :], upto[:, :], colsum[:, :], ALU.subtract))
            link(V_.tensor_tensor(upto[:, :], upto[:, :], psT[:, 0:TT], ALU.add))
            link(V_.tensor_scalar(upto[:, :], upto[:, :], 1.0, 0.0, ALU.subtract, ALU.max))
            link(V_.tensor_copy(last_a[:, :], upto[:, :]))
            last_u = last_row[:, :].bitcast(I32)
            link(V_.tensor_scalar(last_b[:, :], last_a[:, :], P - 1, 4, ALU.bitwise_and, ALU.logical_shift_left))
            V_.tensor_scalar(last_u, last_a[:, :], 7, CH - 1, ALU.logical_shift_right, ALU.bitwise_and)
            link(V_.tensor_scalar(last_a[:, :], last_a[:, :], 11, 11, ALU.logical_shift_right, ALU.logical_shift_left))
            link(V_.tensor_tensor(last_u, last_u, last_b[:, :], ALU.bitwise_or))
            link(V_.tensor_tensor(last_u, last_u, last_a[:, :], ALU.bitwise_or))
            dve.wait_ge(s_x, 32)
            dve.wait_ge(s_param, 16 * (len(ROWS) + len(MATS) + len(EDGE_MATS) + 1))

            def layernorm(dst, src, w=None, b=None, relu=False):
                link(V_.tensor_reduce(mean[:, 0:NT], node(src), AX.X, ALU.add))
                link(V_.tensor_scalar(mean[:, 0:NT], mean[:, 0:NT], 1.0 / D, None, ALU.mult))
                link(V_.tensor_tensor(node(dst), node(src), per_node(mean), ALU.subtract))
                scalar_turn()
                link(V_.tensor_reduce(rstd[:, 0:NT], node(Z), AX.X, ALU.add))
                link(V_.tensor_scalar(rstd[:, 0:NT], rstd[:, 0:NT], 1.0 / D, EPS, ALU.mult, ALU.add))
                scalar_turn()
                link(V_.reciprocal(rstd[:, 0:NT], rstd[:, 0:NT]))
                if relu:
                    link(V_.scalar_tensor_tensor(node(dst), node(dst), 0.0, per_node(rstd), ALU.max, ALU.mult))
                else:
                    link(V_.tensor_tensor(node(dst), node(dst), per_node(rstd), ALU.mult))
                if w is not None:
                    link(V_.tensor_tensor(node(dst), node(dst), per_feature(row(w)), ALU.mult))
                    link(V_.tensor_tensor(node(dst), node(dst), per_feature(row(b)), ALU.add))

            def linear(j, scaled=False):
                dst = LIN[j][2]
                base = NG * j
                dve.sem_inc(s_lin, 1)

                def group(g, b):
                    dve.wait_ge(s_lm, g + (base + 3))
                    to = dst[:, bass.ds(g * GT, GT), :]
                    product = psB[b][:, 0:GT * D].rearrange("p (t d) -> p t d", d=D)
                    if scaled:
                        factor = dinv[:, bass.ds(g * GT, GT)].unsqueeze(2).to_broadcast([P, GT, D])
                        V_.tensor_tensor(to, product, factor, ALU.mult).then_inc(s_lo, 1)
                    else:
                        V_.tensor_copy(to, product).then_inc(s_lo, 1)

                with dve.Fori(0, NG // 2) as i:
                    for b in range(2):
                        group(i * 2 + b, b)
                group(NG - 1, 0)
                dve.wait_ge(s_lo, base + NG + 2)

            def product(k):
                table = H if k == 2 else V
                dve.sem_inc(s_left, 1)
                for part in range(PARTS - 1):
                    for half, (t0, t1) in enumerate(NODE_HALVES):
                        dve.wait_ge(s_cut, 6 * k + 2 * part + half + 1)
                        of = table if part == 0 else Z
                        V_.tensor_tensor(Z[:, t0:t1, :], of[:, t0:t1, :], parts[:, t0:t1, part, :], ALU.subtract
                                         ).then_inc(s_left, 1)

                def tile(i, r, d):
                    dve.wait_ge(s_dag, i * RING + (NT * k + r + RING + 1))
                    V_.tensor_reduce(Z[:, d, :].rearrange("p a d -> p (a d)"),
                                     psF[r % 2][:, 0:PARTS * D].rearrange("p (s d) -> p d s", d=D), AX.X, ALU.add
                                     ).then_inc(s_dev, 1)

                with dve.Fori(0, NT // RING) as i:
                    for r in range(RING):
                        tile(i, r, bass.ds(i * RING + r, 1))
                tile(NT // RING, 0, slice(NT - 1, NT))
                dve.wait_ge(s_dev, NT * (k + 1) + 2)

            def conv(k, meanwhile=None):
                s_, n = conv_sems(k)
                if n == 0:
                    link(V_.memset(scan[:, :, :], 0.0))
                base = 8 * BODIES * n
                op0, op1 = (ALU.add, ALU.max) if KINDS[k] == MAX else (ALU.mult, ALU.add)
                dve.sem_inc(s_.tbl, 1)
                if meanwhile is not None:
                    meanwhile()
                with dve.Fori(0, BODIES) as it:
                    for s in range(SLOTS):
                        h, q, b = s // 4, s % 4, s % 2
                        if q == 0:
                            dve.wait_ge(s_.keep[h], it * 16 + (16 * BODIES * n + 16))
                        dve.wait_ge(s_.fwd, it * 8 + (base + s + 9))
                        dve.wait_ge(s_.back, it * 8 + (base + s + 1))
                        dve.wait_ge(s_.scan, it * 8 + (base + s + 8))
                        V_.tensor_tensor_scan(scan[:, b, :], keep[:, h, q * QUAD:(q + 1) * QUAD], psF[b][0:D, :],
                                              scan[:, 1 - b, QUAD - 1:QUAD], op0, op1).then_inc(s_.scan, 1)
                dve.wait_ge(s_.agg, 16 * NT * (n + 1))
                link(V_.tensor_tensor(node(Z), node(Z), per_node(has_edge), ALU.mult))

            def sums(k):
                before = chained[0]
                with dve.If(mode == 0):
                    conv(k)
                after = chained[0]
                chained[0] = before
                with dve.Else():
                    product(k)
                    dve.sem_inc(s_v, after - chained[0])
                chained[0] = after

            def scale(t):
                link(V_.tensor_tensor(node(t), node(t), per_node(dinv), ALU.mult))

            def add(dst, x, y):
                link(V_.tensor_tensor(node(dst), node(x), node(y), ALU.add))

            def add_row(t, name):
                link(V_.tensor_tensor(node(t), node(t), per_feature(row(name)), ALU.add))

            def gcn(j, k, bias):
                linear(j, scaled=True)
                sums(k)
                add(U, Z, V)
                scale(U)
                add_row(U, bias)

            layernorm(H, X, relu=True)
            layernorm(U, H, "L0_gnn_ln_in_w", "L0_gnn_ln_in_b")
            gcn(0, 0, "L0_gnn_b1")
            link(V_.tensor_scalar(node(U), node(U), 0.0, None, ALU.max))
            gcn(1, 1, "L0_gnn_b2")
            layernorm(H, U, "L0_gnn_ln_out_w", "L0_gnn_ln_out_b")
            add(X, X, H)
            layernorm(H, X, relu=True)
            sums(2)
            link(V_.tensor_scalar(gin_eps[:, :], gin_eps[:, :], 1.0, None, ALU.add))
            link(V_.scalar_tensor_tensor(node(U), node(H), gin_eps[:, 0:1], node(Z), ALU.mult, ALU.add))
            linear(2)
            link(V_.tensor_tensor(node(U), node(V), per_feature(row("L1_gnn_b1")), ALU.add))
            link(V_.tensor_scalar(node(U), node(U), 0.0, None, ALU.max))
            linear(3)
            add_row(V, "L1_gnn_b2")

            def clear_tail(t):
                link(V_.tensor_scalar(t[:, NT - 1, :], t[:, NT - 1, :], real_row[:, 0:1], None, ALU.mult))

            def feature_sums(t, i):
                link(V_.tensor_reduce(bn_a[:, :], node(t).rearrange("p t d -> p d t"), AX.X, ALU.add))
                dve.sem_inc(s_to_pe, 1)
                dve.wait_ge(s_from_pe, i + 1)

            clear_tail(V)
            feature_sums(V, 0)
            link(V_.tensor_scalar(bn_b[:, :], psX[:, 0:D], 1.0 / N, None, ALU.mult))
            link(V_.tensor_tensor(node(V), node(V), per_feature(bn_b[:, :]), ALU.subtract))
            clear_tail(V)
            scalar_turn()
            feature_sums(Z, 1)
            link(V_.tensor_scalar(bn_b[:, :], psX[:, D:2 * D], 1.0 / N, EPS, ALU.mult, ALU.add))
            scalar_turn()
            link(V_.reciprocal(bn_c[:, :], bn_b[:, :]))
            link(V_.tensor_tensor(bn_c[:, :], bn_c[:, :], row("L1_gnn_gamma"), ALU.mult))
            link(V_.tensor_tensor(node(V), node(V), per_feature(bn_c[:, :]), ALU.mult))
            add_row(V, "L1_gnn_beta")
            link(V_.tensor_scalar(node(V), node(V), 0.0, None, ALU.max))
            add(X, X, V)
            layernorm(H, X, relu=True)
            gcn(4, 3, "L2_gnn_b0")
            scalar_turn()
            layernorm(H, U, "L2_gnn_g0", "L2_gnn_be0")
            gcn(5, 4, "L2_gnn_b1")
            scalar_turn()
            layernorm(H, U, "L2_gnn_g1", "L2_gnn_be1")
            add(X, X, H)
            layernorm(H, X, relu=True)
            for i in range(2):
                linear(6 + 2 * i)
                conv(5 + i, meanwhile=lambda: linear(7 + 2 * i))
                add(U, Z, U)
                add_row(U, f"L3_gnn_b{i + 1}")
                link(V_.scalar_tensor_tensor(node(H), node(U), 0.01, node(U), ALU.mult, ALU.max))
            V_.tensor_tensor(node(X), node(X), node(H), ALU.add).then_inc(s_outr, 1)


def kernel(**inputs):
    import numpy as np
    import concourse.bacc as bacc
    from concourse.bass_utils import run_bass_kernel_spmd

    src = np.pad(np.asarray(inputs["src"]), (0, EP - E))
    dst = np.pad(np.asarray(inputs["dst"]), (0, EP - E), constant_values=NT * P - 1)
    ea = np.pad(np.asarray(inputs["edge_attr_32"]), ((0, EP - E), (0, 0)))
    arrays = {name: np.ascontiguousarray(inputs[name]) for name in ["x", "L1_gnn_eps"] + ROWS + MATS + EDGE_MATS}
    arrays["src_chunks"] = np.ascontiguousarray(src.reshape(HALVES, CH, P).transpose(0, 2, 1))
    arrays["dst_chunks"] = np.ascontiguousarray(dst.reshape(HALVES, CH, P).transpose(0, 2, 1))
    arrays["src_line"] = src
    arrays["dst_line"] = dst
    arrays["edge_attr_halves"] = np.ascontiguousarray(ea.reshape(HALVES, HALF, DE).transpose(0, 2, 1))

    nc = bacc.Bacc("TRN2", target_bir_lowering=False, num_devices=1)
    aps = {}
    for name, v in arrays.items():
        dt = U32 if name == "src_chunks" else mybir.dt.from_np(v.dtype)
        aps[name] = nc.dram_tensor(f"in_{name}", v.shape, dt, kind="ExternalInput").ap()
    out = nc.dram_tensor("out_x", (N, D), F32, kind="ExternalOutput").ap()
    gnn_program(nc, aps, out)
    r = run_bass_kernel_spmd(nc, [{f"in_{k}": v for k, v in arrays.items()}], core_ids=[0])
    return r.results[0]["out_x"]
```

```python
from contextlib import ExitStack

import concourse.bass as bass
from concourse import mybir

P = 128
N = 6250
E = 200000
D = 96
DE = 32
NT = (N + P - 1) // P
GT = 4
NG = (NT + GT - 1) // GT
TT = NG * GT
TAIL = N - (NT - 1) * P
QUAD = 4 * P
CH = 16
HALF = CH * P
BODIES = (E + 2 * HALF - 1) // (2 * HALF)
HALVES = 2 * BODIES
EP = HALVES * HALF
SLOTS = 8
EPS = 1e-5
NEG = -3.38e38
SUM, MAX = 0, 1
W = 8
WPT = P // W
WINDOWS = NT * WPT
READ = 3
KEYW = 512
BLOCK = 32
BLOCKS = HALF // BLOCK
PAIR = 2
POOL_LOADS = 4
AGG_GROUPS = 7
TANH_STEPS = 12
AGG_TILES = NT // AGG_GROUPS
ABLK = NT * P
SPLIT = (NT + 1) // 2
RING = 4
PARTS = 2
TOP = 14
LEAST_EXPONENT = 20
assert NT * W <= KEYW and NT % 2 == 1 and READ * P % BLOCK == 0 and NT % RING == 1 and NG % 2 == 1 and NT % AGG_GROUPS == 0 and NT % TANH_STEPS == 1

ALU = mybir.AluOpType
ACT = mybir.ActivationFunctionType
AX = mybir.AxisListType
F32 = mybir.dt.float32
BF16 = mybir.dt.bfloat16
F16 = mybir.dt.float16
I32 = mybir.dt.int32
U32 = mybir.dt.uint32

ROWS = ["L0_gnn_ln_in_w", "L0_gnn_ln_in_b", "L0_gnn_b1", "L0_gnn_b2", "L0_gnn_ln_out_w", "L0_gnn_ln_out_b",
        "L1_gnn_b1", "L1_gnn_b2", "L1_gnn_gamma", "L1_gnn_beta", "L2_gnn_b0", "L2_gnn_g0", "L2_gnn_be0",
        "L2_gnn_b1", "L2_gnn_g1", "L2_gnn_be1", "L3_gnn_b1", "L3_gnn_b2"]
MATS = ["L0_gnn_W1", "L0_gnn_W2", "L1_gnn_W1", "L1_gnn_W2", "L2_gnn_W0", "L2_gnn_W1", "L3_gnn_W1_msg",
        "L3_gnn_W1_root", "L3_gnn_W2_msg", "L3_gnn_W2_root"]
EDGE_MATS = ["L3_gnn_W1_edge", "L3_gnn_W2_edge"]
KINDS = [SUM, SUM, SUM, SUM, SUM, MAX, MAX]


def gnn_program(nc, a, out):
    with ExitStack() as ctx:
        def sb(name, shape, dt=F32):
            return ctx.enter_context(nc.sbuf_tensor(name, shape, dt))

        def ps(name, shape, dt=F32):
            return ctx.enter_context(nc.psum_tensor(name, shape, dt))

        def sem(name):
            return ctx.enter_context(nc.semaphore(name))

        table_d = nc.dram_tensor("table_scratch", (NT * P, D), F32, kind="Internal").ap()
        scan_d = nc.dram_tensor("scan_scratch", (EP, D), F32, kind="Internal").ap()
        flag_d = [nc.dram_tensor(f"flag_scratch_{n}", (HALVES, HALF), BF16, kind="Internal").ap()
                  for n in ("sum", "max")]

        keys_d = nc.dram_tensor("edge_keys_scratch", (EP, 2), F32, kind="Internal").ap()
        adj_d = nc.dram_tensor("adjacency_scratch", (NT * P, ABLK), F16, kind="Internal").ap()

        X = sb("X", [P, TT, D])
        H = sb("H", [P, TT, D])
        U = sb("U", [P, TT, D])
        V = sb("V", [P, TT, D])
        Z = sb("Z", [P, TT, D])
        rows = sb("rows", [P, len(ROWS), D])
        mats = sb("mats", [D, len(MATS), D])
        emats = sb("emats", [DE, 2, D])
        gin_eps = sb("gin_eps", [P, 1])
        iota_i = sb("iota_i", [P, P], I32)
        part_i = sb("part_i", [P, 1], I32)
        iota_f = sb("iota_f", [P, P])
        iota_b = sb("iota_b", [P, P], BF16)
        part_f = sb("part_f", [P, 1])
        ident = sb("ident", [P, P])
        upper = sb("upper", [P, P])
        ones = sb("ones", [P, P])
        real_row = sb("real_row", [P, 1])
        zero_b = sb("zero_b", [P, P], BF16)
        count = sb("count", [P, TT])
        upto = sb("upto", [P, TT])
        colsum = sb("colsum", [P, TT])
        has_edge = sb("has_edge", [P, TT])
        dinv = sb("dinv", [P, TT])
        last_row = sb("last_row", [P, TT], U32)
        last_a = sb("last_a", [P, TT], I32)
        last_b = sb("last_b", [P, TT], I32)
        mean = sb("mean", [P, TT])
        rstd = sb("rstd", [P, TT])
        bn_a = sb("bn_a", [P, D])
        bn_b = sb("bn_b", [P, D])
        bn_c = sb("bn_c", [P, D])
        ones_h = sb("ones_h", [P, 1], F16)
        first_edge = sb("first_edge", [1, WINDOWS], I32)
        first_block = sb("first_block", [1, WINDOWS])
        read_blocks = sb("read_blocks", [1, WINDOWS - 1])
        regular_f = sb("regular_f", [1, 1])
        regular_i = sb("regular_i", [1, 1], I32)
        peaks = sb("peaks", [P, NG])
        peak = sb("peak", [P, 1])
        top = sb("top", [1, 1])
        exponent = sb("exponent", [1, 1])
        exponent_i = sb("exponent_i", [1, 1], I32)
        powers = sb("powers", [1, 2])
        powers_f = sb("powers_f", [1, 2])
        powers_i = sb("powers_i", [1, 2], I32)
        scales = sb("scales", [P, 2])
        stage = sb("stage", [P, 2, GT, D])
        yT = sb("yT", [D, 2, GT * P])

        region = sb("region", [P, (RING * ABLK + NT * PARTS * D) // 2])
        used = [0]

        def carve(parts, shape, dt=F32):
            size = 1
            for n in shape:
                size *= n
            words = size // (2 if dt in (BF16, F16) else 1)
            piece = region[0:parts, used[0]:used[0] + words]
            used[0] += words
            if dt != F32:
                piece = piece.bitcast(dt)
            names = "abcd"[:len(shape)]
            return piece.rearrange(f"p ({' '.join(names)}) -> p {' '.join(names)}",
                                   **{n: v for n, v in zip(names[1:], shape[1:])})

        adj = carve(P, [RING, NT, P], F16)
        parts = carve(P, [NT, PARTS, D], F16)
        used[0] = 0
        idx = carve(P, [2, CH], U32)
        keep = carve(D, [2, HALF], BF16)
        ea = carve(DE, [2, HALF])
        ring = carve(P, [SLOTS * 4, D])
        scan = carve(D, [2, QUAD])
        stored = carve(P, [2, CH, D])
        used[0] = 0
        hot_lo = carve(P, [2, CH, P], BF16)
        hot_hi = carve(P, [2, CH, 64], BF16)
        used[0] = 0
        built = carve(P, [2, NT, P], F16)
        hot_src = carve(P, [4, P, PAIR * READ], F16)
        hot_key = carve(P, [4, READ, NT * W], F16)
        keys = carve(P, [2, WPT * READ, 2])
        own_key = carve(P, [2, WPT * READ])
        place_h16 = carve(P, [2, WPT * READ], F16)
        build_end = used[0]
        window_h = carve(P, [WINDOWS], F16)
        window_key = carve(P, [WINDOWS])
        window_i = carve(P, [WINDOWS], I32)
        window_key_i = carve(P, [WINDOWS], I32)
        place_rep = carve(P, [P, PAIR * READ], F16)
        place_rep_i = carve(P, [P, PAIR * READ], I32)
        later = carve(HALVES, [2, WINDOWS], F16)
        end_i = carve(HALVES, [BLOCKS], I32)
        end_f = carve(HALVES, [BLOCKS])
        place_h = window_h[:, 0:NT * W]
        used[0] = 0
        same = carve(HALVES, [HALF], BF16)
        newseg = carve(HALVES, [HALF], BF16)
        src_i = carve(HALVES, [HALF], I32)
        key_i = carve(HALVES, [HALF], I32)
        key_t = carve(HALVES, [HALF], I32)
        assert used[0] <= build_end
        dst_i = H[:, :, :].rearrange("p t d -> p (t d)").bitcast(I32)[:, 0:HALVES * CH]
        lo_i = H[:, :, :].rearrange("p t d -> p (t d)").bitcast(I32)[:, HALVES * CH:2 * HALVES * CH]
        lo_f = U[:, :, :].rearrange("p t d -> p (t d)")[:, 0:HALVES * CH]
        hi_f = U[:, :, :].rearrange("p t d -> p (t d)")[:, HALVES * CH:2 * HALVES * CH]
        cur_i = V[:, :, :].rearrange("p t d -> p (t d)").bitcast(I32)[0:HALVES, 0:HALF]
        prev_i = V[:, :, :].rearrange("p t d -> p (t d)").bitcast(I32)[0:HALVES, HALF:2 * HALF]
        edge_keys = Z[:, :, :].rearrange("p t d -> p (t d)")[0:HALVES, 0:2 * HALF].rearrange("p (e k) -> p e k", k=2)
        psF = [ps(f"psF{i}", [P, QUAD]) for i in range(2)]
        psB = [ps(f"psB{i}", [P, QUAD]) for i in range(2)]
        psT = ps("psT", [P, QUAD])
        psM = ps("psM", [P, QUAD])
        psX = ps("psX", [P, QUAD])
        banks = [psF[0], psF[1], psB[0], psB[1]]

        s_param = sem("params_loaded")
        s_x = sem("x_loaded")
        s_dst = sem("dst_loaded")
        s_cur = sem("dst_line_loaded")
        s_prev = sem("prev_loaded")
        s_iota = sem("iota_made")
        s_const = sem("consts_made")
        s_flag = sem("flags_made")
        s_flagw = sem("flags_written")
        s_lohi = sem("lo_hi_made")
        s_hot = sem("one_hots_made")
        s_hotu = sem("one_hots_used")
        s_hist = sem("histogram_done")
        s_cnt = sem("count_copied")
        s_pre = sem("prefix_done")
        s_v = sem("vector_chain")
        s_to_act = sem("vector_to_scalar")
        s_from_act = sem("scalar_to_vector")
        s_to_pe = sem("vector_to_tensor")
        s_from_pe = sem("tensor_to_vector")
        s_src = sem("src_loaded")
        s_keys = sem("edge_keys_made")
        s_keysw = sem("edge_keys_written")
        s_later = sem("block_ends_compared")
        s_lateru = sem("block_ends_counted")
        s_regular = sem("path_decided")
        s_peak = sem("peak_or_powers_made")
        s_peakt = sem("peak_turned_or_powers_spread")
        s_tail = sem("step_on_sums_done")
        s_tanh_in = sem("tile_for_tanh_ready")
        s_tanh = sem("tanh_done")
        s_kl = [sem(f"keys_landed_{b}") for b in range(2)]
        s_pkl = [sem(f"keys_landed_by_pool_{b}") for b in range(2)]
        s_prep = sem("window_keys_made_relative")
        s_deg = sem("degrees_done")
        s_hotw = sem("window_one_hots_made")
        s_win = sem("window_counts_done")
        s_wev = sem("window_counts_copied")
        s_ast = [sem(f"adjacency_stored_{h}") for h in range(2)]
        s_at = [sem(f"adjacency_landed_{r}") for r in range(RING)]
        s_scales = sem("table_and_scales_ready")
        s_cut = sem("first_part_rounded")
        s_rest = sem("second_part_rounded")
        s_dag = sem("product_done")
        s_dev = sem("product_summed")
        s_turn = sem("turns")

        class EdgeSems:

            def __init__(self, kind):
                self.tbl = sem(f"{kind}_table_ready")
                self.tblw = sem(f"{kind}_table_written")
                self.idx = [sem(f"{kind}_idx_landed_{h}") for h in range(2)]
                self.keep = [sem(f"{kind}_keep_landed_{h}") for h in range(2)]
                self.ea = [sem(f"{kind}_edge_attr_landed_{h}") for h in range(2)]
                self.g = [sem(f"{kind}_gathered_{s}") for s in range(SLOTS)]
                self.fwd = sem(f"{kind}_feature_major_done")
                self.scan = sem(f"{kind}_scan_done")
                self.back = sem(f"{kind}_edge_major_done")
                self.evac = sem(f"{kind}_edge_major_copied")
                self.st = [sem(f"{kind}_scan_stored_{h}") for h in range(2)]
                self.agg = [sem(f"{kind}_aggregates_landed_{g}") for g in range(AGG_GROUPS)]

        edge_sems = [EdgeSems("sum"), EdgeSems("max")]

        def conv_sems(k):
            return edge_sems[KINDS[k]], k - (5 if KINDS[k] == MAX else 0)

        s_lin = sem("linear_input_ready")
        s_stage = sem("linear_staged")
        s_lt = sem("linear_transposed")
        s_yt = sem("linear_transpose_copied")
        s_lm = sem("linear_product_done")
        s_lo = sem("linear_product_copied")
        s_outr = sem("output_ready")
        s_out = sem("output_stored")

        def node(t):
            return t[:, 0:NT, :]

        def per_node(t):
            return t[:, 0:NT].unsqueeze(2).to_broadcast([P, NT, D])

        def per_feature(t):
            return t.unsqueeze(1).to_broadcast([P, NT, D])

        def row(name):
            return rows[:, ROWS.index(name), :]

        def mat(name):
            return mats[:, MATS.index(name), :]

        LIN = [(U, "L0_gnn_W1", V), (U, "L0_gnn_W2", V), (U, "L1_gnn_W1", V), (V, "L1_gnn_W2", V),
               (H, "L2_gnn_W0", V), (H, "L2_gnn_W1", V), (H, "L3_gnn_W1_msg", V), (H, "L3_gnn_W1_root", U),
               (H, "L3_gnn_W2_msg", V), (H, "L3_gnn_W2_root", U)]
        RELU_IN = (1, 3)
        TANH_OUT = (3, 4)
        NODE_HALVES = [(0, SPLIT), (SPLIT, NT)]
        STEPS = [("lin", 0), ("conv", 0), ("lin", 1), ("conv", 1), ("conv", 2), ("lin", 2), ("lin", 3),
                 ("lin", 4), ("conv", 3), ("lin", 5), ("conv", 4),
                 ("lin", 6), ("lin", 7), ("conv", 5), ("lin", 8), ("lin", 9), ("conv", 6)]

        def adj_tile(d):
            return adj_d.rearrange("(d p) m -> d p m", p=P)[bass.ds(d, 1), :, :].rearrange("a p m -> p (a m)")

        def tile_pairs(eng, step):
            step(0, 0, 0)
            with eng.Fori(0, NT // 2) as i:
                step(i * 2 + 1, 1, i)
                step(i * 2 + 2, 0, i + 1)

        def load_window(eng, d, buf, j, landed):
            first = eng.value_load(first_edge[0:1, bass.ds(d * WPT + j, 1)], min_val=0, max_val=EP - READ * P)
            eng.dma_start(keys[:, buf, j * READ:(j + 1) * READ, :].rearrange("p c k -> p (c k)"),
                          keys_d[bass.ds(first, READ * P), :].rearrange("(p c) k -> p (c k)", c=READ)
                          ).then_inc(landed[buf], 16)

        block = ctx.enter_context(nc.Block())

        @block.sync
        def _(sp):
            sp.dma_start(cur_i, a["dst_line"].rearrange("(h e) -> h e", e=HALF)).then_inc(s_cur, 16)
            sp.dma_start(src_i, a["src_line"].rearrange("(h e) -> h e", e=HALF)).then_inc(s_src, 16)
            sp.wait_ge(s_v, 2)
            sp.dma_start(prev_i[0:1, 1:HALF], a["dst_line"][0:HALF - 1].unsqueeze(0)).then_inc(s_prev, 16)
            sp.dma_start(prev_i[1:HALVES, :], a["dst_line"][HALF - 1:EP - 1].rearrange("(h e) -> h e", e=HALF)
                         ).then_inc(s_prev, 16)
            sp.dma_start(X[:, 0:NT - 1, :], a["x"][0:(NT - 1) * P, :].rearrange("(t p) d -> p t d", p=P)
                         ).then_inc(s_x, 16)
            sp.dma_start(X[0:TAIL, NT - 1, :], a["x"][(NT - 1) * P:N, :]).then_inc(s_x, 16)
            for i, name in enumerate(ROWS):
                sp.dma_start(rows[:, i, :], a[name].partition_broadcast(P)).then_inc(s_param, 16)
            for i, name in enumerate(MATS):
                sp.dma_start(mats[:, i, :], a[name]).then_inc(s_param, 16)
            for i, name in enumerate(EDGE_MATS):
                sp.dma_start(emats[:, i, :], a[name]).then_inc(s_param, 16)
            sp.dma_start(gin_eps[:, :], a["L1_gnn_eps"].partition_broadcast(P)).then_inc(s_param, 16)
            sp.wait_ge(s_flag, 1)
            sp.dma_start(flag_d[SUM], same).then_inc(s_flagw, 16)
            sp.dma_start(flag_d[MAX], newseg).then_inc(s_flagw, 16)
            sp.wait_ge(s_keys, 1)
            sp.dma_start(keys_d.rearrange("(h e) k -> h (e k)", e=HALF), edge_keys.rearrange("p e k -> p (e k)")
                         ).then_inc(s_keysw, 16)
            sp.wait_ge(s_flagw, 32)
            sp.wait_ge(s_keysw, 16)
            sp.wait_ge(s_regular, 1)
            regular = sp.value_load(regular_i[0:1, 0:1], min_val=0, max_val=1)

            def build_loads():
                def load_windows(d, buf, turn):
                    sp.wait_ge(s_prep, d + 1)
                    sp.sem_inc(s_turn, 1)
                    for j in range(POOL_LOADS, WPT):
                        load_window(sp, d, buf, j, s_kl)

                tile_pairs(sp, load_windows)
                sp.wait_ge(s_ast[0], 16 * (NT // 2 + 2))
                sp.wait_ge(s_ast[1], 16 * (NT // 2 + 1))
                sp.wait_ge(s_deg, NT + 2)

            with sp.If(regular == 1):
                build_loads()

            def product_loads(k):
                sp.wait_ge(s_dag, NT * k + RING)
                with sp.Fori(0, NT // RING) as i:
                    for r in range(RING):
                        d = sp.snap(i * RING + r)
                        sp.wait_ge(s_dag, i * RING + (NT * k + r + 1))
                        sp.sem_inc(s_turn, 1)
                        sp.dma_start(adj[:, r, :, :].rearrange("p t c -> p (t c)"), adj_tile(d)
                                     ).then_inc(s_at[r], 16)
                sp.wait_ge(s_dag, NT * k + NT)
                sp.dma_start(adj[:, 0, :, :].rearrange("p t c -> p (t c)"), adj_tile(NT - 1)
                             ).then_inc(s_at[0], 16)

            def conv_loads(k):
                kind = KINDS[k]
                s_, n = conv_sems(k)
                base = 8 * BODIES * n
                sp.wait_ge(s_.tbl, n + 1)
                sp.dma_start(table_d.rearrange("(t p) d -> p t d", p=P), node(H if k == 2 else V)
                             ).then_inc(s_.tblw, 16)
                with sp.Fori(0, BODIES) as it:
                    for h in range(2):
                        half = sp.snap(it * 2 + h)
                        sp.wait_ge(s_.fwd, it * 8 + (base + 4 * h + 4))
                        sp.wait_ge(s_.scan, it * 8 + (base + 4 * h + 4))
                        sp.sem_inc(s_turn, 1)
                        sp.dma_start(idx[:, h, :], a["src_chunks"][bass.ds(half, 1), :, :].rearrange("a p c -> p (a c)")
                                     ).then_inc(s_.idx[h], 16)
                        sp.dma_start(keep[:, h, :], flag_d[kind][bass.ds(half, 1), :].rearrange("a e -> (a e)")
                                     .partition_broadcast(D)).then_inc(s_.keep[h], 16)
                        if kind == MAX:
                            sp.dma_start(ea[:, h, :], a["edge_attr_halves"][bass.ds(half, 1), :, :].rearrange(
                                "a f e -> f (a e)")).then_inc(s_.ea[h], 16)

            with sp.If(regular == 1):
                for k in range(5):
                    product_loads(k)
            with sp.Else():
                sp.dma_start(dst_i, a["dst_chunks"].rearrange("h p c -> p h c")).then_inc(s_dst, 16)
                for k in range(5):
                    conv_loads(k)
            for k in (5, 6):
                conv_loads(k)
            for g in range(AGG_GROUPS):
                t0 = g * AGG_TILES
                t1 = min(t0 + AGG_TILES, NT - 1)
                sp.wait_ge(s_outr, g + 1)
                sp.dma_start(out[t0 * P:t1 * P, :].rearrange("(t p) d -> p t d", p=P), X[:, t0:t1, :]
                             ).then_inc(s_out, 16)
            sp.dma_start(out[(NT - 1) * P:N, :], X[0:TAIL, NT - 1, :]).then_inc(s_out, 16)
            sp.wait_ge(s_out, 16 * (AGG_GROUPS + 1))

        @block.gpsimd
        def _(pool):
            nc.gpsimd.iota(iota_i[:, :], pattern=[[1, P]], base=0, channel_multiplier=0).then_inc(s_iota, 1)
            nc.gpsimd.iota(part_i[:, :], pattern=[[0, 1]], base=0, channel_multiplier=1).then_inc(s_iota, 1)
            nc.gpsimd.iota(window_i, pattern=[[1, WINDOWS]], base=0, channel_multiplier=0).then_inc(s_iota, 1)
            nc.gpsimd.iota(window_key_i, pattern=[[KEYW, WINDOWS]], base=0, channel_multiplier=0).then_inc(s_iota, 1)
            nc.gpsimd.iota(place_rep_i, pattern=[[1, P], [0, PAIR * READ]], base=0, channel_multiplier=0
                           ).then_inc(s_iota, 1)
            pool.sem_inc(s_prep, 2)
            pool.wait_ge(s_regular, 1)
            regular = pool.value_load(regular_i[0:1, 0:1], min_val=0, max_val=1)

            def load_windows(d, buf):
                pool.wait_ge(s_prep, d + 1)
                pool.sem_inc(s_turn, 1)
                for j in range(POOL_LOADS):
                    load_window(pool, d, buf, j, s_pkl)

            def relative_keys(d, buf, turn):
                pool.wait_ge(s_kl[buf], turn * (16 * (WPT - POOL_LOADS)) + 16 * (WPT - POOL_LOADS))
                pool.wait_ge(s_pkl[buf], turn * (16 * POOL_LOADS) + 16 * POOL_LOADS)
                pool.wait_ge(s_hotw, d * WPT + WPT)
                pool.sem_inc(s_turn, 1)
                own_window = window_key[:, bass.ds(d * WPT, WPT)].unsqueeze(2).to_broadcast([P, WPT, READ])
                nc.gpsimd.tensor_tensor(own_key[:, buf, :].rearrange("p (j c) -> p j c", c=READ),
                                        keys[:, buf, :, 0].rearrange("p (j c) -> p j c", c=READ),
                                        own_window, ALU.subtract)
                nc.gpsimd.tensor_copy(place_h16[:, buf, :], keys[:, buf, :, 1]).then_inc(s_prep, 1)

            with pool.If(regular == 1):
                load_windows(0, 0)
                with pool.Fori(0, NT // 2) as i:
                    load_windows(i * 2 + 1, 1)
                    relative_keys(i * 2, 0, i)
                    load_windows(i * 2 + 2, 0)
                    relative_keys(i * 2 + 1, 1, i)
                relative_keys(NT - 1, 0, NT // 2)

            def gathers(k):
                s_, n = conv_sems(k)
                pool.wait_ge(s_.tblw, 16 * (n + 1))
                with pool.Fori(0, BODIES) as it:
                    for h in range(2):
                        pool.wait_ge(s_.idx[h], it * 16 + (16 * BODIES * n + 16))
                        pool.wait_ge(s_.fwd, it * 8 + (8 * BODIES * n + 4 * h + 4))
                        pool.sem_inc(s_turn, 1)
                        for c in range(CH):
                            nc.gpsimd.indirect_dma_start(
                                ring[:, h * CH + c, :], None, table_d,
                                bass.IndirectOffsetOnAxis(ap=idx[:, h, c:c + 1], axis=0)
                            ).then_inc(s_.g[4 * h + c // 4], 16)
                pool.wait_ge(s_.st[0], 16 * (BODIES * (n + 1) + 1))
                pool.wait_ge(s_.st[1], 16 * (BODIES * (n + 1) + 1))
                for t in range(NT):
                    nc.gpsimd.indirect_dma_start(
                        Z[:, t, :], None, scan_d, bass.IndirectOffsetOnAxis(ap=last_row[:, t:t + 1], axis=0)
                    ).then_inc(s_.agg[t // AGG_TILES], 16)

            with pool.If(regular == 0):
                for k in range(5):
                    gathers(k)
            for k in (5, 6):
                gathers(k)

        @block.tensor
        def _(pe):
            for s_ in edge_sems:
                pe.sem_inc(s_.fwd, 8)
                pe.sem_inc(s_.back, 2)
            pe.sem_inc(s_win, 4)
            pe.sem_inc(s_deg, 2)
            pe.sem_inc(s_lateru, 2)
            pe.sem_inc(s_dag, RING)
            pe.sem_inc(s_hotu, 2)
            pe.sem_inc(s_lt, 2)
            pe.sem_inc(s_lm, 2)
            pe.wait_ge(s_const, 1)
            half_w = WINDOWS // 2

            def count_blocks(c, b, start, stop):
                pe.wait_ge(s_later, c + 1)
                for bank in range(2):
                    last = nc.tensor.matmul(psF[bank][0:1, 0:half_w], ones_h[0:HALVES, :],
                                            later[:, b, bank * half_w:(bank + 1) * half_w], start=start, stop=stop)
                last.then_inc(s_lateru, 1)

            count_blocks(0, 0, True, False)
            with pe.Fori(0, BLOCKS // 2 - 1) as i:
                count_blocks(i * 2 + 1, 1, False, False)
                count_blocks(i * 2 + 2, 0, False, False)
            count_blocks(BLOCKS - 1, 1, False, True)
            pe.wait_ge(s_regular, 1)
            regular = pe.value_load(regular_i[0:1, 0:1], min_val=0, max_val=1)

            def build():
                def degrees(d, buf):
                    pe.wait_ge(s_wev, d * WPT + (WPT + 4))
                    for t in range(NT):
                        last = nc.tensor.matmul(psX[:, bass.ds(d, 1)], built[:, buf, t, :], ones_h[:, :],
                                                start=(t == 0), stop=(t == NT - 1))
                    last.then_inc(s_deg, 1)

                def count_windows(d, buf, before=None):
                    for j in range(WPT):
                        pe.wait_ge(s_hotw, d * WPT + (j + 2 * WPT + 1))
                        pe.wait_ge(s_wev, d * WPT + (j + 1))
                        for c in range(READ):
                            last = nc.tensor.matmul(banks[j % 4][:, 0:NT * W],
                                                    hot_src[:, j // PAIR % 4, :, j % PAIR * READ + c],
                                                    hot_key[:, j % 4, c, :],
                                                    start=(c == 0), stop=(c == READ - 1))
                        last.then_inc(s_win, 1)
                        if j == WPT // 2 and before is not None:
                            degrees(before, 1 - buf)

                count_windows(0, 0)
                with pe.Fori(0, NT // 2) as i:
                    count_windows(i * 2 + 1, 1, i * 2)
                    count_windows(i * 2 + 2, 0, i * 2 + 1)
                degrees(NT - 1, 0)

            def histogram():
                hist = psX[:, 0:64]
                nc.tensor.matmul(hist, zero_b[:, :], zero_b[:, 0:64], start=True, stop=False)
                with pe.Fori(0, BODIES) as it:
                    for h in range(2):
                        pe.wait_ge(s_hot, it * 2 + (h + 1))
                        for c in range(CH):
                            last = nc.tensor.matmul(hist, hot_lo[:, h, c, :], hot_hi[:, h, c, :], start=False,
                                                    stop=False)
                        last.then_inc(s_hotu, 1)
                nc.tensor.matmul(hist, zero_b[:, :], zero_b[:, 0:64], start=False, stop=True).then_inc(s_hist, 1)

            with pe.If(regular == 1):
                build()
            with pe.If(regular == 0):
                histogram()
            pe.wait_ge(s_cnt, 1)
            nc.tensor.matmul(psT[:, 0:TT], upper[:, :], count[:, :], start=True, stop=True)
            nc.tensor.matmul(psM[:, 0:TT], ones[:, :], count[:, :], start=True, stop=True).then_inc(s_pre, 1)

            def product(k):
                pe.wait_ge(s_peak, 2 * k + 1)
                nc.tensor.transpose(psT[0:1, 0:P], peak[:, :], ident[:, :]).then_inc(s_peakt, 1)
                pe.wait_ge(s_peak, 2 * k + 2)
                nc.tensor.matmul(psM[:, 0:2], ones[0:1, :], powers[:, :], start=True, stop=True).then_inc(s_peakt, 1)
                pe.wait_ge(s_rest, 2 * (k + 1))

                def tile(i, r, landed):
                    pe.wait_ge(s_at[r], landed)
                    pe.wait_ge(s_dev, i * RING + (NT * k + r + 1))
                    for t in range(NT):
                        last = nc.tensor.matmul(psF[r % 2][:, 0:PARTS * D], adj[:, r, t, :],
                                                parts[:, t, :, :].rearrange("p s d -> p (s d)"),
                                                start=(t == 0), stop=(t == NT - 1))
                    last.then_inc(s_dag, 1)

                full = NT // RING
                with pe.Fori(0, full) as i:
                    for r in range(RING):
                        tile(i, r, i * 16 + 16 * ((full + (r == 0)) * k + 1))
                tile(full, 0, 16 * (full + 1) * (k + 1))

            def linear(j):
                src, w, dst = LIN[j]
                base = NG * j

                def turn(g, b):
                    pe.wait_ge(s_stage, g + (base + 1))
                    pe.wait_ge(s_yt, g + (base + 1))
                    for t in range(GT):
                        last = nc.tensor.transpose(psF[b][0:D, t * P:(t + 1) * P], stage[:, b, t, :], ident[:, :])
                    last.then_inc(s_lt, 1)

                def multiply(g, b):
                    pe.wait_ge(s_yt, g + (base + 3))
                    pe.wait_ge(s_lo, g + (base + 1))
                    for t in range(GT):
                        last = nc.tensor.matmul(psB[b][:, t * D:(t + 1) * D], yT[:, b, t * P:(t + 1) * P], mat(w),
                                                start=True, stop=True)
                    last.then_inc(s_lm, 1)

                turn(0, 0)
                with pe.Fori(0, NG // 2) as i:
                    turn(i * 2 + 1, 1)
                    multiply(i * 2, 0)
                    turn(i * 2 + 2, 0)
                    multiply(i * 2 + 1, 1)
                multiply(NG - 1, 0)
                pe.wait_ge(s_lo, base + NG + 2)

            def conv(k):
                s_, n = conv_sems(k)
                base = 8 * BODIES * n

                def feature_major(it, s):
                    h, q, b = s // 4, s % 4, s % 2
                    pe.wait_ge(s_.scan, it * 8 + (base + s + 7))
                    pe.wait_ge(s_.g[s], it * 64 + (64 * BODIES * n + 64))
                    if KINDS[k] == MAX:
                        pe.wait_ge(s_.ea[h], it * 16 + (16 * BODIES * n + 16))
                        nc.tensor.matmul(psF[b][0:D, :], emats[:, n, :], ea[:, h, q * QUAD:(q + 1) * QUAD],
                                         start=True, stop=False)
                    for c in range(4):
                        rows_in = ring[:, 4 * s + c, :]
                        if KINDS[k] == MAX:
                            last = nc.tensor.matmul(psF[b][0:D, c * P:(c + 1) * P], rows_in, ident[:, :],
                                                    start=False, stop=(c == 3))
                        else:
                            last = nc.tensor.transpose(psF[b][0:D, c * P:(c + 1) * P], rows_in, ident[:, :])
                    last.then_inc(s_.fwd, 1)

                def edge_major(it, s):
                    b = s % 2
                    pe.wait_ge(s_.scan, it * 8 + (base + s + 9))
                    pe.wait_ge(s_.evac, it * 8 + (base + s + 1))
                    for c in range(4):
                        last = nc.tensor.transpose(psB[b][:, c * D:(c + 1) * D], scan[:, b, c * P:(c + 1) * P],
                                                   ident[0:D, 0:D])
                    last.then_inc(s_.back, 1)

                with pe.Fori(0, BODIES) as it:
                    feature_major(it, 0)
                    for s in range(SLOTS):
                        if s + 1 < SLOTS:
                            feature_major(it, s + 1)
                        edge_major(it, s)

            pe.wait_ge(s_param, 16 * (len(ROWS) + len(MATS) + len(EDGE_MATS) + 1))
            for what, n in STEPS:
                if what == "lin":
                    linear(n)
                elif KINDS[n] == MAX:
                    conv(n)
                else:
                    with pe.If(regular == 1):
                        product(n)
                    with pe.Else():
                        conv(n)
                if (what, n) == ("lin", 3):
                    for i in range(2):
                        pe.wait_ge(s_to_pe, i + 1)
                        nc.tensor.matmul(psX[:, i * D:(i + 1) * D], ones[:, :], bn_a[:, :], start=True, stop=True
                                         ).then_inc(s_from_pe, 1)

        @block.scalar
        def _(act):
            for s_ in edge_sems:
                act.sem_inc(s_.evac, 2)
                act.sem_inc(s_.st[0], 16)
                act.sem_inc(s_.st[1], 16)
            act.sem_inc(s_wev, 4)
            act.sem_inc(s_yt, 2)
            act.sem_inc(s_ast[0], 16)
            act.sem_inc(s_ast[1], 16)
            handed = [0]

            def from_vector(call):
                handed[0] += 1
                act.wait_ge(s_to_act, handed[0])
                call().then_inc(s_from_act, 1)

            def by_halves(to, t, function):
                for t0, t1 in NODE_HALVES:
                    from_vector(lambda: nc.scalar.activation(to[:, t0:t1, :], t[:, t0:t1, :], function))

            def root():
                from_vector(lambda: nc.scalar.activation(rstd[:, 0:NT], rstd[:, 0:NT], ACT.Sqrt))

            def square_and_root(t):
                by_halves(Z, t, ACT.Square)
                root()

            def linear(j):
                src, w, dst = LIN[j]
                base = NG * j
                function = ACT.Relu if j in RELU_IN else ACT.Copy
                act.wait_ge(s_lin, j + 1)

                def stage_group(g, b):
                    act.wait_ge(s_lt, g + (base + 1))
                    nc.scalar.activation(stage[:, b, :, :], src[:, bass.ds(g * GT, GT), :], function
                                         ).then_inc(s_stage, 1)

                def copy_turned(g, b):
                    act.wait_ge(s_lt, g + (base + 3))
                    act.wait_ge(s_lm, g + (base + 1))
                    nc.scalar.copy(yT[:, b, :], psF[b][0:D, :]).then_inc(s_yt, 1)

                stage_group(0, 0)
                with act.Fori(0, NG // 2) as i:
                    stage_group(i * 2 + 1, 1)
                    copy_turned(i * 2, 0)
                    stage_group(i * 2 + 2, 0)
                    copy_turned(i * 2 + 1, 1)
                copy_turned(NG - 1, 0)

            def cut(k):
                table = H if k == 2 else V
                act.wait_ge(s_scales, k + 1)
                for t0, t1 in NODE_HALVES:
                    nc.scalar.activation(parts[:, t0:t1, 0, :], table[:, t0:t1, :], ACT.Copy, scale=scales[:, 0:1]
                                         ).then_inc(s_cut, 1)

            def build():
                def collect(d, buf, turn):
                    act.wait_ge(s_ast[buf], turn * 16 + 16)
                    act.wait_ge(s_deg, d + 1)
                    for j in range(WPT):
                        act.wait_ge(s_win, d * WPT + (j + 5))
                        nc.scalar.copy(built[:, buf, :, j * W:(j + 1) * W],
                                       banks[j % 4][:, 0:NT * W].rearrange("p (t w) -> p t w", w=W)).then_inc(s_wev, 1)
                    act.wait_ge(s_wev, d * WPT + (WPT + 4))
                    act.dma_start(adj_tile(d), built[:, buf, :, :].rearrange("p t c -> p (t c)")
                                  ).then_inc(s_ast[buf], 16)

                tile_pairs(act, collect)

            def conv(k):
                s_, n = conv_sems(k)
                base = 8 * BODIES * n
                with act.Fori(0, BODIES) as it:
                    for s in range(SLOTS):
                        h, q, b = s // 4, s % 4, s % 2
                        if q == 0:
                            act.wait_ge(s_.st[h], it * 16 + (16 * BODIES * n + 16))
                        act.wait_ge(s_.back, it * 8 + (base + s + 3))
                        nc.scalar.copy(stored[:, h, q * 4:(q + 1) * 4, :],
                                       psB[b][:, 0:4 * D].rearrange("p (c d) -> p c d", d=D)).then_inc(s_.evac, 1)
                        if q == 3:
                            act.wait_ge(s_.evac, it * 8 + (base + s + 3))
                            act.dma_start(
                                scan_d.rearrange("(i p c) d -> i p (c d)", p=P, c=CH)[bass.ds(it * 2 + h, 1), :, :]
                                .rearrange("a p m -> p (a m)"),
                                stored[:, h, :, :].rearrange("p c d -> p (c d)")).then_inc(s_.st[h], 16)

            act.wait_ge(s_regular, 1)
            regular = act.value_load(regular_i[0:1, 0:1], min_val=0, max_val=1)
            with act.If(regular == 1):
                build()
            from_vector(lambda: nc.scalar.activation(dinv[:, 0:NT], dinv[:, 0:NT], ACT.Sqrt))

            def sums(k):
                with act.If(regular == 1):
                    cut(k)
                with act.Else():
                    conv(k)
                if k in TANH_OUT:
                    base = NT * TANH_OUT.index(k)

                    def tanh_tile(d):
                        act.wait_ge(s_tanh_in, d + (base + 1))
                        nc.scalar.activation(U[:, bass.ds(d, 1), :], U[:, bass.ds(d, 1), :], ACT.Tanh
                                             ).then_inc(s_tanh, 1)

                    with act.Fori(0, NT // TANH_STEPS) as i:
                        for r in range(TANH_STEPS):
                            tanh_tile(i * TANH_STEPS + r)
                    tanh_tile(NT - 1)

            square_and_root(H)
            square_and_root(U)
            linear(0)
            sums(0)
            linear(1)
            sums(1)
            root()
            square_and_root(H)
            sums(2)
            linear(2)
            linear(3)
            from_vector(lambda: nc.scalar.activation(node(Z), node(V), ACT.Square))
            from_vector(lambda: nc.scalar.activation(bn_b[:, :], bn_b[:, :], ACT.Sqrt))
            square_and_root(H)
            linear(4)
            sums(3)
            root()
            linear(5)
            sums(4)
            root()
            square_and_root(H)
            for i in range(2):
                linear(6 + 2 * i)
                linear(7 + 2 * i)
                conv(5 + i)

        @block.vector
        def _(dve):
            chained, handed, to_pe = [0], [0], [0]
            V_ = nc.vector

            def link(ins):
                chained[0] += 1
                ins.then_inc(s_v, 1)
                dve.wait_ge(s_v, chained[0])

            def scalar_turn():
                handed[0] += 1
                dve.sem_inc(s_to_act, 1)
                dve.wait_ge(s_from_act, handed[0])

            link(V_.memset(prev_i[0:1, 0:1], -1))
            link(V_.memset(X[:, NT - 1:TT, :], 0.0))
            for t in (H, U, V):
                V_.memset(t[:, NT:TT, :], 0.0)
            for s_ in edge_sems:
                dve.sem_inc(s_.scan, 8)
            dve.sem_inc(s_hotw, 2 * WPT)
            dve.sem_inc(s_dev, 2)
            dve.sem_inc(s_lo, 2)
            V_.memset(zero_b[:, :], 0.0)
            V_.memset(ones[:, :], 1.0)
            V_.memset(ones_h[:, :], 1.0)
            dve.wait_ge(s_iota, 5)
            V_.tensor_copy(window_h, window_i)
            V_.tensor_copy(place_rep, place_rep_i)
            V_.tensor_copy(window_key, window_key_i)
            V_.tensor_copy(iota_f[:, :], iota_i[:, :])
            V_.tensor_copy(iota_b[:, :], iota_i[:, :])
            link(V_.tensor_copy(part_f[:, :], part_i[:, :]))
            V_.tensor_scalar(ident[:, :], iota_f[:, :], part_f[:, 0:1], None, ALU.is_equal)
            V_.tensor_scalar(upper[:, :], iota_f[:, :], part_f[:, 0:1], None, ALU.is_ge)
            V_.tensor_scalar(real_row[:, :], part_f[:, :], float(TAIL), None, ALU.is_lt).then_inc(s_const, 1)
            window_bits, key_bits, place_bits = W.bit_length() - 1, KEYW.bit_length() - 1, 7
            dve.wait_ge(s_cur, 16)
            ends = cur_i.rearrange("p (b e) -> p b e", e=BLOCK)
            link(V_.tensor_scalar(end_i, ends[:, :, BLOCK - 1], window_bits, None, ALU.logical_shift_right))
            link(V_.tensor_copy(end_f, end_i))

            def compare_blocks(c, b):
                dve.wait_ge(s_lateru, c + 1)
                V_.tensor_scalar(later[:, b, :], window_h[0:HALVES, :], end_f[:, bass.ds(c, 1)], None, ALU.is_gt
                                 ).then_inc(s_later, 1)

            with dve.Fori(0, BLOCKS // 2) as i:
                for b in range(2):
                    compare_blocks(i * 2 + b, b)
            dve.wait_ge(s_lateru, BLOCKS + 2)
            half_w = WINDOWS // 2
            for bank in range(2):
                link(V_.tensor_copy(first_block[:, bank * half_w:(bank + 1) * half_w], psF[bank][0:1, 0:half_w]))
            V_.tensor_scalar(first_edge[:, :], first_block[:, :], float(BLOCK), float(EP - READ * P), ALU.mult, ALU.min)
            link(V_.tensor_tensor(read_blocks[:, :], first_block[:, 1:WINDOWS], first_block[:, 0:WINDOWS - 1],
                                  ALU.subtract))
            link(V_.tensor_reduce(regular_f[:, :], read_blocks[:, :], AX.X, ALU.max))
            link(V_.tensor_scalar(regular_f[:, :], regular_f[:, :], float(READ * P // BLOCK - 1), None, ALU.is_le))
            link(V_.tensor_copy(regular_i[:, :], regular_f[:, :]))
            dve.wait_ge(s_prev, 32)
            link(V_.tensor_tensor(same, cur_i, prev_i, ALU.is_equal))
            V_.tensor_scalar(newseg, same, -NEG, NEG, ALU.mult, ALU.add).then_inc(s_flag, 1)
            dve.wait_ge(s_src, 16)
            link(V_.tensor_scalar(key_i, cur_i, window_bits, key_bits, ALU.logical_shift_right,
                                  ALU.logical_shift_left))
            link(V_.tensor_scalar(key_t, cur_i, W - 1, None, ALU.bitwise_and))
            link(V_.tensor_tensor(key_i, key_i, key_t, ALU.bitwise_or))
            link(V_.tensor_scalar(key_t, src_i, place_bits, window_bits, ALU.logical_shift_right,
                                  ALU.logical_shift_left))
            link(V_.tensor_tensor(key_i, key_i, key_t, ALU.bitwise_or))
            link(V_.tensor_copy(edge_keys[:, :, 0], key_i))
            link(V_.tensor_scalar(key_t, src_i, P - 1, None, ALU.bitwise_and))
            V_.tensor_copy(edge_keys[:, :, 1], key_t).then_inc(s_keys, 1)
            dve.wait_ge(s_flagw, 32)
            dve.wait_ge(s_keysw, 16)
            dve.sem_inc(s_regular, 1)
            regular = dve.value_load(regular_i[0:1, 0:1], min_val=0, max_val=1)

            def build():
                def one_hots(d, buf, turn):
                    dve.wait_ge(s_prep, d + 3)
                    for j in range(WPT):
                        dve.wait_ge(s_win, d * WPT + (j + 1))
                        if j % PAIR == 0:
                            places = place_h16[:, buf, j * READ:(j + PAIR) * READ].unsqueeze(1)
                            V_.tensor_tensor(hot_src[:, j // PAIR % 4, :, :], place_rep,
                                             places.to_broadcast([P, P, PAIR * READ]), ALU.is_equal)
                        for c in range(READ):
                            e = j * READ + c
                            last = V_.tensor_scalar(hot_key[:, j % 4, c, :], place_h, own_key[:, buf, e:e + 1], None,
                                                    ALU.is_equal)
                        last.then_inc(s_hotw, 1)

                tile_pairs(dve, one_hots)
                dve.wait_ge(s_deg, NT + 2)
                V_.memset(count[:, NT:TT], 0.0)
                link(V_.tensor_copy(count[:, 0:NT], psX[:, 0:NT]))
                dve.wait_ge(s_ast[0], 16 * (NT // 2 + 2))
                dve.wait_ge(s_ast[1], 16 * (NT // 2 + 1))

            def histogram():
                link(V_.memset(hot_hi, 0.0))
                dve.wait_ge(s_dst, 16)
                link(V_.tensor_scalar(lo_i, dst_i, P - 1, None, ALU.bitwise_and))
                link(V_.tensor_copy(lo_f, lo_i))
                link(V_.tensor_scalar(lo_i, dst_i, 7, None, ALU.logical_shift_right))
                link(V_.tensor_copy(hi_f, lo_i))
                with dve.Fori(0, BODIES) as it:
                    for h in range(2):
                        dve.wait_ge(s_hotu, it * 2 + (h + 1))
                        for c in range(CH):
                            e = it * (2 * CH) + (h * CH + c)
                            V_.tensor_scalar(hot_lo[:, h, c, :], iota_b[:, :], lo_f[:, bass.ds(e, 1)], None,
                                             ALU.is_equal)
                            last = V_.tensor_scalar(hot_hi[:, h, c, 0:TT], iota_b[:, 0:TT], hi_f[:, bass.ds(e, 1)],
                                                    None, ALU.is_equal)
                        last.then_inc(s_hot, 1)
                dve.wait_ge(s_hist, 1)
                link(V_.tensor_copy(count[:, :], psX[:, 0:TT]))

            before = chained[0]
            with dve.If(regular == 0):
                histogram()
            after = chained[0]
            chained[0] = before
            with dve.Else():
                build()
                dve.sem_inc(s_v, after - chained[0])
            chained[0] = after
            dve.sem_inc(s_cnt, 1)
            V_.tensor_scalar(has_edge[:, :], count[:, :], 0.0, None, ALU.is_gt)
            link(V_.tensor_scalar(dinv[:, :], count[:, :], 1.0, None, ALU.add))
            scalar_turn()
            V_.reciprocal(dinv[:, 0:NT], dinv[:, 0:NT])
            dve.wait_ge(s_pre, 1)
            link(V_.tensor_copy(colsum[:, :], psM[:, 0:TT]))
            link(V_.tensor_tensor_scan(upto[:, :], ones[:, 0:TT], colsum[:, :], 0.0, ALU.mult, ALU.add))
            link(V_.tensor_tensor(upto[:, :], upto[:, :], colsum[:, :], ALU.subtract))
            link(V_.tensor_tensor(upto[:, :], upto[:, :], psT[:, 0:TT], ALU.add))
            link(V_.tensor_scalar(upto[:, :], upto[:, :], 1.0, 0.0, ALU.subtract, ALU.max))
            link(V_.tensor_copy(last_a[:, :], upto[:, :]))
            last_u = last_row[:, :].bitcast(I32)
            link(V_.tensor_scalar(last_b[:, :], last_a[:, :], P - 1, 4, ALU.bitwise_and, ALU.logical_shift_left))
            V_.tensor_scalar(last_u, last_a[:, :], 7, CH - 1, ALU.logical_shift_right, ALU.bitwise_and)
            link(V_.tensor_scalar(last_a[:, :], last_a[:, :], 11, 11, ALU.logical_shift_right, ALU.logical_shift_left))
            link(V_.tensor_tensor(last_u, last_u, last_b[:, :], ALU.bitwise_or))
            link(V_.tensor_tensor(last_u, last_u, last_a[:, :], ALU.bitwise_or))
            dve.wait_ge(s_x, 32)
            dve.wait_ge(s_param, 16 * (len(ROWS) + len(MATS) + len(EDGE_MATS) + 1))

            def layernorm(dst, src, w=None, b=None, relu=False):
                link(V_.tensor_reduce(mean[:, 0:NT], node(src), AX.X, ALU.add))
                link(V_.tensor_scalar(mean[:, 0:NT], mean[:, 0:NT], 1.0 / D, None, ALU.mult))
                for t0, t1 in NODE_HALVES:
                    link(V_.tensor_tensor(dst[:, t0:t1, :], src[:, t0:t1, :],
                                          mean[:, t0:t1].unsqueeze(2).to_broadcast([P, t1 - t0, D]), ALU.subtract))
                    dve.sem_inc(s_to_act, 1)
                for t0, t1 in NODE_HALVES:
                    handed[0] += 1
                    dve.wait_ge(s_from_act, handed[0])
                    link(V_.tensor_reduce(rstd[:, t0:t1], Z[:, t0:t1, :], AX.X, ALU.add))
                normalize(dst, w, b, relu)

            def normalize(dst, w, b, relu=False):
                link(V_.tensor_scalar(rstd[:, 0:NT], rstd[:, 0:NT], 1.0 / D, EPS, ALU.mult, ALU.add))
                scalar_turn()
                link(V_.reciprocal(rstd[:, 0:NT], rstd[:, 0:NT]))
                if relu:
                    link(V_.scalar_tensor_tensor(node(dst), node(dst), 0.0, per_node(rstd), ALU.max, ALU.mult))
                else:
                    link(V_.tensor_tensor(node(dst), node(dst), per_node(rstd), ALU.mult))
                if w is not None:
                    link(V_.tensor_tensor(node(dst), node(dst), per_feature(row(w)), ALU.mult))
                    link(V_.tensor_tensor(node(dst), node(dst), per_feature(row(b)), ALU.add))

            def linear(j, scaled=False, bias=None):
                dst = LIN[j][2]
                base = NG * j
                dve.sem_inc(s_lin, 1)

                def group(g, b):
                    dve.wait_ge(s_lm, g + (base + 3))
                    to = dst[:, bass.ds(g * GT, GT), :]
                    product = psB[b][:, 0:GT * D].rearrange("p (t d) -> p t d", d=D)
                    if scaled:
                        factor = dinv[:, bass.ds(g * GT, GT)].unsqueeze(2).to_broadcast([P, GT, D])
                        V_.tensor_tensor(to, product, factor, ALU.mult).then_inc(s_lo, 1)
                    elif bias is not None:
                        V_.tensor_tensor(to, product, row(bias).unsqueeze(1).to_broadcast([P, GT, D]), ALU.add
                                         ).then_inc(s_lo, 1)
                    else:
                        V_.tensor_copy(to, product).then_inc(s_lo, 1)
                    if scaled:
                        dve.wait_ge(s_lo, g + (base + 3))
                        return V_.tensor_reduce(peaks[:, bass.ds(g, 1)], to, AX.XY, ALU.max, apply_absolute_value=True)

                with dve.Fori(0, NG // 2) as i:
                    for b in range(2):
                        group(i * 2 + b, b)
                last = group(NG - 1, 0)
                if scaled:
                    link(last)
                dve.wait_ge(s_lo, base + NG + 2)

            def gcn_tail(bias):
                def steps(d, tiles):
                    return [lambda: V_.scalar_tensor_tensor(U[:, tiles, :], Z[:, tiles, :], scales[:, 1:2],
                                                            V[:, tiles, :], ALU.mult, ALU.add),
                            lambda: V_.scalar_tensor_tensor(U[:, tiles, :], U[:, tiles, :], dinv[:, d],
                                                            row(bias).unsqueeze(1), ALU.mult, ALU.add)]
                return steps

            def gin_tail():
                def steps(d, tiles):
                    return [lambda: V_.tensor_scalar(Z[:, tiles, :], Z[:, tiles, :], scales[:, 1:2], None, ALU.mult),
                            lambda: V_.scalar_tensor_tensor(U[:, tiles, :], H[:, tiles, :], gin_eps[:, 0:1],
                                                            Z[:, tiles, :], ALU.mult, ALU.add)]
                return steps

            def center():
                def steps(d, tiles):
                    return [lambda: V_.tensor_reduce(mean[:, d], U[:, tiles, :], AX.X, ALU.add),
                            lambda: V_.tensor_scalar(mean[:, d], mean[:, d], 1.0 / D, None, ALU.mult),
                            lambda: V_.tensor_scalar(H[:, tiles, :], U[:, tiles, :], mean[:, d], None, ALU.subtract),
                            lambda: V_.tensor_tensor(Z[:, tiles, :], H[:, tiles, :], H[:, tiles, :], ALU.mult),
                            lambda: V_.tensor_reduce(rstd[:, d], Z[:, tiles, :], AX.X, ALU.add)]
                return steps

            TANH = None
            taken = [0]

            def steps_on(k, tails):
                per_tile = sum(1 if tail is TANH else len(tail(0, 0)) for tail in tails) - (TANH in tails)
                base = taken[0]

                def step(i, r, d):
                    at = base + r * per_tile
                    for tail in tails:
                        if tail is TANH:
                            dve.sem_inc(s_tanh_in, 1)
                            dve.wait_ge(s_tanh, i * RING + (NT * TANH_OUT.index(k) + r + 1))
                            continue
                        for op in tail(d, d):
                            at += 1
                            op().then_inc(s_tail, 1)
                            dve.wait_ge(s_tail, i * (RING * per_tile) + at)
                return step, per_tile

            def product(k, step):
                table = H if k == 2 else V
                if k == 2:
                    link(V_.tensor_reduce(peak[:, :], node(table), AX.XY, ALU.max, apply_absolute_value=True))
                else:
                    link(V_.tensor_reduce(peak[:, :], peaks[:, :], AX.X, ALU.max))
                dve.sem_inc(s_peak, 1)
                dve.wait_ge(s_peakt, 2 * k + 1)
                link(V_.tensor_reduce(top[:, :], psT[0:1, 0:P], AX.X, ALU.max))
                link(V_.tensor_scalar(exponent_i[:, :], top[:, :].bitcast(I32), 23, None, ALU.logical_shift_right))
                link(V_.tensor_copy(exponent[:, :], exponent_i[:, :]))
                link(V_.tensor_scalar(exponent[:, :], exponent[:, :], float(LEAST_EXPONENT), None, ALU.max))
                V_.tensor_scalar(powers_f[:, 0:1], exponent[:, :], -1.0, float(254 + TOP), ALU.mult, ALU.add)
                link(V_.tensor_scalar(powers_f[:, 1:2], exponent[:, :], float(TOP), None, ALU.subtract))
                link(V_.tensor_copy(powers_i[:, :], powers_f[:, :]))
                link(V_.tensor_scalar(powers[:, :].bitcast(I32), powers_i[:, :], 23, None, ALU.logical_shift_left))
                dve.sem_inc(s_peak, 1)
                dve.wait_ge(s_peakt, 2 * k + 2)
                link(V_.tensor_copy(scales[:, :], psM[:, 0:2]))
                dve.sem_inc(s_scales, 1)
                for half, (t0, t1) in enumerate(NODE_HALVES):
                    dve.wait_ge(s_cut, 2 * k + half + 1)
                    V_.scalar_tensor_tensor(parts[:, t0:t1, 1, :], table[:, t0:t1, :], scales[:, 0:1],
                                            parts[:, t0:t1, 0, :], ALU.mult, ALU.subtract).then_inc(s_rest, 1)

                def tile(i, r, d):
                    done = i * RING + (NT * k + r + 1)
                    dve.wait_ge(s_dag, done + RING)
                    V_.tensor_reduce(Z[:, d, :].rearrange("p a d -> p (a d)"),
                                     psF[r % 2][:, 0:PARTS * D].rearrange("p (s d) -> p d s", d=D), AX.X, ALU.add
                                     ).then_inc(s_dev, 1)
                    dve.wait_ge(s_dev, done + 2)
                    step(i, r, d)

                with dve.Fori(0, NT // RING) as i:
                    for r in range(RING):
                        tile(i, r, bass.ds(i * RING + r, 1))
                tile(NT // RING, 0, slice(NT - 1, NT))

            def conv(k, meanwhile=None, and_then=None):
                s_, n = conv_sems(k)
                if n == 0:
                    link(V_.memset(scan[:, :, :], 0.0))
                base = 8 * BODIES * n
                op0, op1 = (ALU.add, ALU.max) if KINDS[k] == MAX else (ALU.mult, ALU.add)
                dve.sem_inc(s_.tbl, 1)
                if meanwhile is not None:
                    meanwhile()
                with dve.Fori(0, BODIES) as it:
                    for s in range(SLOTS):
                        h, q, b = s // 4, s % 4, s % 2
                        if q == 0:
                            dve.wait_ge(s_.keep[h], it * 16 + (16 * BODIES * n + 16))
                        dve.wait_ge(s_.fwd, it * 8 + (base + s + 9))
                        dve.wait_ge(s_.back, it * 8 + (base + s + 1))
                        dve.wait_ge(s_.scan, it * 8 + (base + s + 8))
                        V_.tensor_tensor_scan(scan[:, b, :], keep[:, h, q * QUAD:(q + 1) * QUAD], psF[b][0:D, :],
                                              scan[:, 1 - b, QUAD - 1:QUAD], op0, op1).then_inc(s_.scan, 1)
                for g in range(AGG_GROUPS):
                    tiles = slice(g * AGG_TILES, (g + 1) * AGG_TILES)
                    dve.wait_ge(s_.agg[g], 16 * AGG_TILES * (n + 1))
                    link(V_.tensor_tensor(Z[:, tiles, :], Z[:, tiles, :],
                                          has_edge[:, tiles].unsqueeze(2).to_broadcast([P, AGG_TILES, D]), ALU.mult))
                    if and_then is not None:
                        and_then(tiles)

            def sums(k, *tails):
                step, per_tile = steps_on(k, tails)
                before = chained[0]
                with dve.If(regular == 1):
                    product(k, step)
                after = chained[0]
                chained[0] = before
                with dve.Else():
                    conv(k)
                    link(V_.memset(scales[:, :], 1.0))
                    with dve.Fori(0, NT // RING) as i:
                        for r in range(RING):
                            step(i, r, bass.ds(i * RING + r, 1))
                    step(NT // RING, 0, slice(NT - 1, NT))
                    if after > chained[0]:
                        dve.sem_inc(s_v, after - chained[0])
                assert after >= chained[0]
                chained[0] = after
                taken[0] += NT * per_tile

            def add(dst, x, y):
                link(V_.tensor_tensor(node(dst), node(x), node(y), ALU.add))

            def add_row(t, name):
                link(V_.tensor_tensor(node(t), node(t), per_feature(row(name)), ALU.add))

            def gcn(j, k, bias, *then):
                linear(j, scaled=True)
                sums(k, gcn_tail(bias), *then)

            layernorm(H, X, relu=True)
            layernorm(U, H, "L0_gnn_ln_in_w", "L0_gnn_ln_in_b")
            gcn(0, 0, "L0_gnn_b1")
            gcn(1, 1, "L0_gnn_b2", center())
            normalize(H, "L0_gnn_ln_out_w", "L0_gnn_ln_out_b")
            add(X, X, H)
            layernorm(H, X, relu=True)
            link(V_.tensor_scalar(gin_eps[:, :], gin_eps[:, :], 1.0, None, ALU.add))
            sums(2, gin_tail())
            linear(2, bias="L1_gnn_b1")
            linear(3, bias="L1_gnn_b2")

            def clear_tail(t):
                link(V_.tensor_scalar(t[:, NT - 1, :], t[:, NT - 1, :], real_row[:, 0:1], None, ALU.mult))

            def feature_sums(t, i):
                link(V_.tensor_reduce(bn_a[:, :], node(t).rearrange("p t d -> p d t"), AX.X, ALU.add))
                dve.sem_inc(s_to_pe, 1)
                dve.wait_ge(s_from_pe, i + 1)

            clear_tail(V)
            feature_sums(V, 0)
            link(V_.tensor_scalar(bn_b[:, :], psX[:, 0:D], 1.0 / N, None, ALU.mult))
            link(V_.tensor_tensor(node(V), node(V), per_feature(bn_b[:, :]), ALU.subtract))
            clear_tail(V)
            scalar_turn()
            feature_sums(Z, 1)
            link(V_.tensor_scalar(bn_b[:, :], psX[:, D:2 * D], 1.0 / N, EPS, ALU.mult, ALU.add))
            scalar_turn()
            link(V_.reciprocal(bn_c[:, :], bn_b[:, :]))
            link(V_.tensor_tensor(bn_c[:, :], bn_c[:, :], row("L1_gnn_gamma"), ALU.mult))
            link(V_.tensor_tensor(node(V), node(V), per_feature(bn_c[:, :]), ALU.mult))
            add_row(V, "L1_gnn_beta")
            link(V_.scalar_tensor_tensor(node(X), node(V), 0.0, node(X), ALU.max, ALU.add))
            layernorm(H, X, relu=True)
            gcn(4, 3, "L2_gnn_b0", TANH, center())
            normalize(H, "L2_gnn_g0", "L2_gnn_be0")
            gcn(5, 4, "L2_gnn_b1", TANH, center())
            normalize(H, "L2_gnn_g1", "L2_gnn_be1")
            add(X, X, H)
            layernorm(H, X, relu=True)
            for i in range(2):
                def root_and_bias():
                    linear(7 + 2 * i, bias=f"L3_gnn_b{i + 1}")

                def layer_end(tiles):
                    link(V_.tensor_tensor(U[:, tiles, :], Z[:, tiles, :], U[:, tiles, :], ALU.add))
                    link(V_.scalar_tensor_tensor(H[:, tiles, :], U[:, tiles, :], 0.01, U[:, tiles, :],
                                                 ALU.mult, ALU.max))
                    if i == 1:
                        V_.tensor_tensor(X[:, tiles, :], X[:, tiles, :], H[:, tiles, :], ALU.add).then_inc(s_outr, 1)

                linear(6 + 2 * i)
                conv(5 + i, meanwhile=root_and_bias, and_then=layer_end)


def kernel(**inputs):
    import numpy as np
    import concourse.bacc as bacc
    from concourse.bass_utils import run_bass_kernel_spmd

    src = np.pad(np.asarray(inputs["src"]), (0, EP - E))
    dst = np.pad(np.asarray(inputs["dst"]), (0, EP - E), constant_values=NT * P - 1)
    ea = np.pad(np.asarray(inputs["edge_attr_32"]), ((0, EP - E), (0, 0)))
    arrays = {name: np.ascontiguousarray(inputs[name]) for name in ["x", "L1_gnn_eps"] + ROWS + MATS + EDGE_MATS}
    arrays["src_chunks"] = np.ascontiguousarray(src.reshape(HALVES, CH, P).transpose(0, 2, 1))
    arrays["dst_chunks"] = np.ascontiguousarray(dst.reshape(HALVES, CH, P).transpose(0, 2, 1))
    arrays["src_line"] = src
    arrays["dst_line"] = dst
    arrays["edge_attr_halves"] = np.ascontiguousarray(ea.reshape(HALVES, HALF, DE).transpose(0, 2, 1))

    nc = bacc.Bacc("TRN2", target_bir_lowering=False, num_devices=1)
    aps = {}
    for name, v in arrays.items():
        dt = U32 if name == "src_chunks" else mybir.dt.from_np(v.dtype)
        aps[name] = nc.dram_tensor(f"in_{name}", v.shape, dt, kind="ExternalInput").ap()
    out = nc.dram_tensor("out_x", (N, D), F32, kind="ExternalOutput").ap()
    gnn_program(nc, aps, out)
    r = run_bass_kernel_spmd(nc, [{f"in_{k}": v for k, v in arrays.items()}], core_ids=[0])
    return r.results[0]["out_x"]
```
